# Optimizing a Trainium2 kernel written in Bass

```python
import numpy as np
import jax
import jax.numpy as jnp

def _softmax(x, axis=-1):
    return jax.nn.softmax(x, axis=axis)

def _gelu(x):
    return jax.nn.gelu(x, approximate=True)

def _silu(x):
    return jax.nn.silu(x)

def _sigmoid(x):
    return jax.nn.sigmoid(x)

def _layernorm(x, axis=-1, eps=1e-05):
    m = jnp.mean(x, axis=axis, keepdims=True)
    v = jnp.var(x, axis=axis, keepdims=True)
    return (x - m) / jnp.sqrt(v + eps)

def _scatter_add(tgt, idx, src, axis=0):
    return tgt.at[idx].add(src)

def _segment_sum(src, seg, n):
    return jax.ops.segment_sum(src, seg, n)
kernel_name = 'mk_decoder_postln_d1_seqx_r4_a54934'

def setup_inputs(seed: int=0):
    np.random.seed(seed)
    _w = jnp.asarray

    def _rec_inputs():
        import jax
        import jax.numpy as jnp
        _rk = jax.random.key(seed)
        x = -0.0003929 + 0.9999 * jax.random.normal(jax.random.fold_in(_rk, 1), (32, 256, 256), jnp.float32)
        _lenS = 256 - jax.random.randint(jax.random.fold_in(_rk, 7), (32,), 0, max(1, 256 // 4) + 1, jnp.int32)
        _lenS2 = 77 - jax.random.randint(jax.random.fold_in(_rk, 8), (32,), 0, max(1, 77 // 4) + 1, jnp.int32)
        _ctx_1024P = jax.random.normal(jax.random.fold_in(_rk, 11), (32, 16, 256), jnp.float32)
        _ctx_1024c = jax.random.dirichlet(jax.random.fold_in(_rk, 511), 0.3 * jnp.ones((16,), jnp.float32), (32, 77))
        _ctx_1024t = jnp.einsum('bsk,bkd->bsd', _ctx_1024c, _ctx_1024P)
        _ctx_1024t = _ctx_1024t * jax.lax.rsqrt(jnp.mean(jnp.square(_ctx_1024t)) + 1e-12) * 0.953939
        ctx_1024 = -1.39393e-06 + 0.999914 * (_ctx_1024t + 0.3 * jax.random.normal(jax.random.fold_in(_rk, 611), (32, 77, 256), jnp.float32))
        return (x, ctx_1024)
    x, ctx_1024 = _rec_inputs()

    def _L0_attn_setup():
        import jax, jax.numpy as jnp
        import numpy as np
        N_HEAD = 16
        D_HEAD = 64
        D_MODEL = 256
        SEQ = 512
        BATCH = 2
        key = jax.random.key(seed)
        k1, k2, k3, k4 = jax.random.split(key, 4)
        s = 1.0 / np.sqrt(D_MODEL)
        return {'h': jax.random.normal(k1, (SEQ, BATCH, D_MODEL), dtype=jnp.float32), 'Wq': jax.random.normal(k2, (D_MODEL, N_HEAD * D_HEAD), dtype=jnp.float32) * s, 'Wkv': jax.random.normal(k3, (D_MODEL, 2 * N_HEAD * D_HEAD), dtype=jnp.float32) * s, 'Wo': jax.random.normal(k4, (N_HEAD * D_HEAD, D_MODEL), dtype=jnp.float32) * s}
    _L0_attn_all = _L0_attn_setup()
    _L0_attn_in = {k: v for k, v in _L0_attn_all.items() if k in ('Wq', 'Wkv', 'Wo')}
    del _L0_attn_all

    def _L0_xattn_setup():
        import jax, jax.numpy as jnp
        import numpy as np
        B, C_LEN, Q_LEN, D = (8, 512, 128, 256)
        key = jax.random.key(seed)
        ks = jax.random.split(key, 10)
        scale = 1.0 / np.sqrt(D)
        return {'c': jax.random.normal(ks[0], (B, C_LEN, D), dtype=jnp.float32), 'q': jax.random.normal(ks[1], (B, Q_LEN, D), dtype=jnp.float32), 'w_cq': jax.random.normal(ks[2], (D,), dtype=jnp.float32) * scale, 'b_cq': jax.random.normal(ks[3], (), dtype=jnp.float32) * scale, 'w_c': jax.random.normal(ks[4], (D,), dtype=jnp.float32) * scale, 'b_c': jax.random.normal(ks[5], (), dtype=jnp.float32) * scale, 'w_q': jax.random.normal(ks[6], (D,), dtype=jnp.float32) * scale, 'b_q': jax.random.normal(ks[7], (), dtype=jnp.float32) * scale, 'W_l': jax.random.normal(ks[8], (D, 4 * D), dtype=jnp.float32) * (1.0 / np.sqrt(4 * D)), 'b_l': jax.random.normal(ks[9], (D,), dtype=jnp.float32) * (1.0 / np.sqrt(4 * D))}
    _L0_xattn_all = _L0_xattn_setup()
    _L0_xattn_in = {k: v for k, v in _L0_xattn_all.items() if k in ('w_cq', 'b_cq', 'w_c', 'b_c', 'w_q', 'b_q', 'W_l', 'b_l')}
    del _L0_xattn_all

    def _L0_ffn_setup():
        import jax, jax.numpy as jnp
        import numpy as np
        D_MODEL = 256
        DEPTH = 8
        M = 2 ** DEPTH
        N_INTERNAL = M - 1
        B, T = (8, 1024)

        def _leaf_probs(gate):
            BT = gate.shape[0]
            lp = jnp.ones((BT, M), dtype=gate.dtype)
            for level in range(DEPTH):
                n = 2 ** level
                half = M // (2 * n)
                g = gate[:, n - 1:2 * n - 1]
                f = jnp.stack([1.0 - g, g], axis=-1)
                f = jnp.broadcast_to(f[..., None], (BT, n, 2, half))
                lp = lp * f.reshape(BT, M)
            return lp
        key = jax.random.key(seed)
        ks = jax.random.split(key, 7)
        x = jax.random.normal(ks[0], (B, T, D_MODEL), dtype=jnp.float32)
        Wq = jax.random.normal(ks[1], (D_MODEL, D_MODEL), dtype=jnp.float32) * 0.02
        routers = jax.random.normal(ks[2], (N_INTERNAL, D_MODEL), dtype=jnp.float32) * 0.02
        leaf_keys = jax.random.normal(ks[3], (M, D_MODEL), dtype=jnp.float32) * 0.02
        leaf_values = jax.random.normal(ks[4], (M, D_MODEL), dtype=jnp.float32) * 0.02
        Wout_w = jax.random.normal(ks[5], (D_MODEL, D_MODEL), dtype=jnp.float32) * 0.02
        Wout_b = jax.random.normal(ks[6], (D_MODEL,), dtype=jnp.float32) * 0.02
        return {'x': x, 'Wq': Wq, 'routers': routers, 'leaf_keys': leaf_keys, 'leaf_values': leaf_values, 'Wout_w': Wout_w, 'Wout_b': Wout_b}
    _L0_ffn_all = _L0_ffn_setup()
    _L0_ffn_in = {k: v for k, v in _L0_ffn_all.items() if k in ('Wq', 'routers', 'leaf_keys', 'leaf_values', 'Wout_w', 'Wout_b')}
    del _L0_ffn_all
    return {'x': x, 'ctx_1024': ctx_1024, 'L0_attn_Wq': _L0_attn_in['Wq'], 'L0_attn_Wkv': _L0_attn_in['Wkv'], 'L0_attn_Wo': _L0_attn_in['Wo'], 'L0_xattn_w_cq': _L0_xattn_in['w_cq'], 'L0_xattn_b_cq': _L0_xattn_in['b_cq'], 'L0_xattn_w_c': _L0_xattn_in['w_c'], 'L0_xattn_b_c': _L0_xattn_in['b_c'], 'L0_xattn_w_q': _L0_xattn_in['w_q'], 'L0_xattn_b_q': _L0_xattn_in['b_q'], 'L0_xattn_W_l': _L0_xattn_in['W_l'], 'L0_xattn_b_l': _L0_xattn_in['b_l'], 'L0_ffn_Wq': _L0_ffn_in['Wq'], 'L0_ffn_routers': _L0_ffn_in['routers'], 'L0_ffn_leaf_keys': _L0_ffn_in['leaf_keys'], 'L0_ffn_leaf_values': _L0_ffn_in['leaf_values'], 'L0_ffn_Wout_w': _L0_ffn_in['Wout_w'], 'L0_ffn_Wout_b': _L0_ffn_in['Wout_b']}

def reference(x, ctx_1024, L0_attn_Wq, L0_attn_Wkv, L0_attn_Wo, L0_xattn_w_cq, L0_xattn_b_cq, L0_xattn_w_c, L0_xattn_b_c, L0_xattn_w_q, L0_xattn_b_q, L0_xattn_W_l, L0_xattn_b_l, L0_ffn_Wq, L0_ffn_routers, L0_ffn_leaf_keys, L0_ffn_leaf_values, L0_ffn_Wout_w, L0_ffn_Wout_b):
    import jax
    import jax.numpy as jnp

    def _L0_attn_ref(h, Wq, Wkv, Wo):
        import jax, jax.numpy as jnp
        import numpy as np
        N_HEAD = 16
        D_HEAD = 64
        D_MODEL = 256
        SEQ = 512
        BATCH = 2
        L, B, _ = h.shape
        scale = 1.0 / np.sqrt(D_HEAD).astype(np.float32)
        q = (h @ Wq).reshape(L, B, N_HEAD, D_HEAD)
        k, v = jnp.split(h @ Wkv, 2, axis=-1)
        k = k.reshape(L, B, N_HEAD, D_HEAD)
        v = v.reshape(L, B, N_HEAD, D_HEAD)
        score = jnp.einsum('ibnd,jbnd->ijbn', q, k) * scale
        prob = jax.nn.softmax(score, axis=1)
        vec = jnp.einsum('ijbn,jbnd->ibnd', prob, v).reshape(L, B, N_HEAD * D_HEAD)
        return vec @ Wo

    def _L0_xattn_ref(c, q, w_cq, b_cq, w_c, b_c, w_q, b_q, W_l, b_l):
        import jax, jax.numpy as jnp
        import numpy as np
        B, C_LEN, Q_LEN, D = (8, 512, 128, 256)
        cq = jnp.einsum('bcd,bqd,d->bcq', c, q, w_cq) + b_cq
        s = (c @ w_c + b_c)[:, :, None] + (q @ w_q + b_q)[:, None, :] + cq
        a = jax.nn.softmax(s, axis=2)
        c2q_att = jnp.einsum('bcq,bqd->bcd', a, q)
        b_att = jax.nn.softmax(jnp.max(s, axis=2), axis=1)
        q2c_att = jnp.einsum('bc,bcd->bd', b_att, c)[:, None, :]
        x = jnp.concatenate([c, c2q_att, c * c2q_att, c * q2c_att], axis=-1)
        z = x @ W_l.T + b_l
        return z

    def _L0_ffn_ref(x, Wq, routers, leaf_keys, leaf_values, Wout_w, Wout_b):
        import jax, jax.numpy as jnp
        import numpy as np
        D_MODEL = 256
        DEPTH = 8
        M = 2 ** DEPTH
        N_INTERNAL = M - 1
        B, T = (8, 1024)

        def _leaf_probs(gate):
            BT = gate.shape[0]
            lp = jnp.ones((BT, M), dtype=gate.dtype)
            for level in range(DEPTH):
                n = 2 ** level
                half = M // (2 * n)
                g = gate[:, n - 1:2 * n - 1]
                f = jnp.stack([1.0 - g, g], axis=-1)
                f = jnp.broadcast_to(f[..., None], (BT, n, 2, half))
                lp = lp * f.reshape(BT, M)
            return lp
        Bv, Tv, d = x.shape
        q = jnp.einsum('btd,ed->bte', x, Wq)
        q_flat = q.reshape(Bv * Tv, d)
        gate = jax.nn.sigmoid(q_flat @ routers.T)
        leaf_prob = _leaf_probs(gate)
        ret = (leaf_prob @ leaf_values).reshape(Bv, Tv, d)
        return jnp.einsum('btd,ed->bte', ret, Wout_w) + Wout_b
    x = _layernorm(x + _L0_attn_ref(x, L0_attn_Wq, L0_attn_Wkv, L0_attn_Wo), axis=-1)
    x = _layernorm(x + _L0_xattn_ref(x, ctx_1024, L0_xattn_w_cq, L0_xattn_b_cq, L0_xattn_w_c, L0_xattn_b_c, L0_xattn_w_q, L0_xattn_b_q, L0_xattn_W_l, L0_xattn_b_l), axis=-1)
    x = _layernorm(x + _L0_ffn_ref(x, L0_ffn_Wq, L0_ffn_routers, L0_ffn_leaf_keys, L0_ffn_leaf_values, L0_ffn_Wout_w, L0_ffn_Wout_b), axis=-1)
    return x

_drawn_inputs = setup_inputs


def setup_inputs(seed=0):
    import zlib

    import numpy as np

    out = dict(_drawn_inputs(seed))
    spreads = {}
    factors = {'L0_ffn_Wq': 8.0,
     'L0_ffn_routers': 8.0,
     'L0_ffn_leaf_values': 8.0,
     'L0_ffn_Wout_w': 8.0,
     'L0_ffn_Wout_b': 2.725}
    for name, (base, spread) in spreads.items():
        noise = np.random.default_rng([zlib.crc32(name.encode()), seed]).standard_normal(out[name].shape)
        drawn = base * np.exp(spread * noise) if base else spread * noise
        out[name] = jnp.asarray(drawn.astype(out[name].dtype))
    for name, factor in factors.items():
        out[name] = (out[name] * factor).astype(out[name].dtype)
    return out
```

```python
from contextlib import ExitStack

import concourse.bass as bass
from concourse import mybir

F32 = mybir.dt.float32
F32R = mybir.dt.float32r
ALU = mybir.AluOpType
ACT = mybir.ActivationFunctionType
AX = mybir.AxisListType

P = 128
L = 32
NB = 256
D = 256
KT = D // P
NH = 16
DH = 64
HD = NH * DH
HC = HD // P
GB = P // L
SGT = 2
TOK = SGT * P
NSG = L * NB // TOK
NPROJ = 12
NQ = 77
LEAVES = 256
DEPTH = 8
EPS = 1e-5
SCORE_SCALE = DH ** -0.5
NX = SGT * GB


def above_zero(value):
    return not isinstance(value, int) or value > 0


def begun(b):
    return not isinstance(b, int) or b >= 0


def live(b):
    return not isinstance(b, int) or 0 <= b < L


def count(b):
    return min(b + 1, L) if isinstance(b, int) else b + 1


def f(ap):
    return ap.bitcast(F32)


def decoder_layer(nc, x, ctx_in, Wq, Wkv, Wo, w_cq, b_cq, w_c, b_c, w_q, b_q, WlT, b_l, fWq, routersT, leafT,
                  WoutT, Wout_b, out):
    with ExitStack() as top:
        def sem(name):
            return top.enter_context(nc.semaphore(name))

        yT = top.enter_context(nc.sbuf_tensor("yT", [P, KT, L * NB], F32))
        ident = top.enter_context(nc.sbuf_tensor("ident", [P, P], F32))
        neg_half = top.enter_context(nc.sbuf_tensor("neg_half", [P, 2], F32))
        s_ident0, s_ident = sem("ident_zeroed"), sem("ident_ready")
        attention(nc, sem, x, Wq, Wkv, Wo, yT, ident, neg_half, s_ident0, s_ident)
        cross_and_tree(nc, sem, ctx_in, w_cq, b_cq, w_c, b_c, w_q, b_q, WlT, b_l, fWq, routersT, leafT, WoutT,
                       Wout_b, yT, ident, neg_half, s_ident, out)


def attention(nc, sem, x, Wq, Wkv, Wo, yT, ident, neg_half, s_ident0, s_ident):
    with ExitStack() as ctx:
        def sb(name, shape, dt=F32):
            return ctx.enter_context(nc.sbuf_tensor(name, shape, dt))

        w_hi = sb("w_hi", [P, 3, KT, HD], F32R)
        w_lo = sb("w_lo", [P, 3, KT, HD], F32R)
        wo_hi = sb("wo_hi", [P, HC, D], F32R)
        wo_lo = sb("wo_lo", [P, HC, D], F32R)
        xT_hi = sb("xT_hi", [P, KT, TOK], F32R)
        xT_lo = sb("xT_lo", [P, KT, TOK], F32R)
        x_nat = [sb(f"x_nat{u}", [P, SGT, D]) for u in range(2)]
        qT = [sb(f"qT{u}", [P, HC, TOK]) for u in range(2)]
        kT = [sb(f"kT{u}", [P, HC, TOK]) for u in range(2)]
        v = [sb(f"v{u}", [P, SGT, HD]) for u in range(2)]
        prob = sb("prob", [P, NH, L])
        prob4 = prob[:].rearrange("p (r n) j -> p r n j", r=2)
        probT = sb("probT", [P, NH, P])
        rowmax = sb("rowmax", [P, NH])
        rowsum = sb("rowsum", [P, NH])
        rowinv = sb("rowinv", [P, NH])
        vecT_hi = sb("vecT_hi", [P, HC, P], F32R)
        vecT_lo = sb("vecT_lo", [P, HC, P], F32R)
        x_res = [sb(f"x_res{g}", [P, D]) for g in range(SGT)]
        res = sb("res", [P, D])
        y_nat = sb("y_nat", [P, D])
        stats = sb("stats", [P, 6])
        mv = sb("mv", [P, 2])
        veps = sb("veps", [P, 1])
        rstd = sb("rstd", [P, 1])

        wl, wsplit_hi, wsplit_lo, zeroed = sem("w_loaded"), sem("weights_hi_done"), sem("weights_lo_done"), sem("probT_zeroed")
        raw = [qT[0], kT[0], qT[1], kT[1]]
        with nc.Block() as block:
            @block.sync
            def _(sp):
                for j, src in enumerate((Wq, Wkv[:, 0:HD], Wkv[:, HD:2 * HD])):
                    sp.dma_start(raw[j][:].rearrange("p c t -> p (c t)").rearrange("p (k n) -> p k n", k=KT),
                                 src.rearrange("(k p) n -> p k n", p=P)).then_inc(wl, 16)
                sp.dma_start(raw[3][:], Wo.rearrange("(c p) n -> p c n", p=P)).then_inc(wl, 16)

            @block.scalar
            def _(act):
                act.wait_ge(wl, 64)
                for j in range(3):
                    act.activation(w_hi[:, j], raw[j][:].rearrange("p c t -> p (c t)").rearrange(
                        "p (k n) -> p k n", k=KT), ACT.Copy).then_inc(wsplit_hi, 1)
                act.activation(wo_hi[:], raw[3][:], ACT.Copy).then_inc(wsplit_hi, 1)

            @block.vector
            def _(dve):
                dve.memset(probT[:], 0.0).then_inc(zeroed, 1)
                dve.memset(neg_half[:], -0.5).then_inc(zeroed, 1)
                for j in range(3):
                    dve.wait_ge(wsplit_hi, j + 1)
                    dve.tensor_tensor(w_lo[:, j], raw[j][:].rearrange("p c t -> p (c t)").rearrange(
                        "p (k n) -> p k n", k=KT), f(w_hi[:, j]), ALU.subtract).then_inc(wsplit_lo, 1)
                dve.wait_ge(wsplit_hi, 4)
                dve.tensor_tensor(wo_lo[:], raw[3][:], f(wo_hi[:]), ALU.subtract).then_inc(wsplit_lo, 1)

            @block.gpsimd
            def _(pool):
                pool.memset(ident[:], 0.0).then_inc(s_ident0, 1)
                pool.wait_ge(s_ident0, 1)
                pool.affine_select(out=ident[:], in_=ident[:], compare_op=ALU.not_equal, fill=1.0, base=0,
                                   pattern=[[-1, P]], channel_multiplier=1).then_inc(s_ident, 1)

        def ps(name, shape):
            return ctx.enter_context(nc.psum_tensor(name, shape, F32))

        xT_ps = ps("xT_ps", [P, KT, TOK])
        proj_ps = [ps(f"proj_ps{u}", [P, 512]) for u in range(2)]
        score_ps = ps("score_ps", [P, 2, 512])
        s_view = score_ps[:, :, 0:NH // 2 * L].rearrange("p r (n j) -> p r n j", j=L)
        vecT_ps = ps("vecT_ps", [P, HC, P])
        oy_ps = ps("oy_ps", [P, 2, D])
        o_ps = oy_ps[:, 0, :]
        yT_ps = oy_ps[:, 1, :].rearrange("p (k t) -> p k t", k=KT)

        x_in = [sem(f"x_in{u}") for u in range(2)]
        res_in = [sem(f"res_in{g}") for g in range(SGT)]
        xT_done, xhi_done, xlo_done = sem("xT_done"), sem("xhi_done"), sem("xlo_done")
        proj_done, evac_act, evac_dve = sem("proj_done"), sem("evac_act"), sem("evac_dve")
        score_done, max_done, sub_done, exp_done = sem("score_done"), sem("max_done"), sem("sub_done"), sem("exp_done")
        sum_done, inv_done, prob_done, probT_done = sem("sum_done"), sem("inv_done"), sem("prob_done"), sem("probT_done")
        pv_done, vhi_done, vlo_done, o_done = sem("pv_done"), sem("vhi_done"), sem("vlo_done"), sem("o_done")
        res_done, st_done, mv_done, eps_done = sem("res_done"), sem("st_done"), sem("mv_done"), sem("eps_done")
        rstd_done, y_done, ytr_done, yT_done = sem("rstd_done"), sem("y_done"), sem("ytr_done"), sem("yT_done")

        def steps(eng, step):
            step(0, 0, 0, 2)
            step(1, 1, 0, 2)
            with eng.Fori(1, NSG // 2 - 1) as pair:
                step(pair * 2, 0, pair, 2)
                step(pair * 2 + 1, 1, pair, 2)
            step(NSG - 2, 0, NSG // 2 - 1, 1)
            step(NSG - 1, 1, NSG // 2 - 1, 0)

        with nc.Block() as block:
            @block.sync
            def _(sp):
                def load(s, u):
                    if above_zero(s - 1):
                        sp.wait_ge(xT_done, s - 1)
                    for g in range(SGT):
                        columns(x_nat[u][:, g, :], s, g, x_in[u])

                def columns(dst, s, g, landed):
                    for b in range(GB):
                        col = s * (SGT * GB) + (g * GB + b)
                        sp.dma_start(dst[b * L:(b + 1) * L, :], x[:, bass.ds(col, 1), :].rearrange(
                            "i a d -> i (a d)")).then_inc(landed, 16)

                def load_res(s):
                    for g in range(SGT):
                        if above_zero((s - 1) * SGT + g + 1):
                            sp.wait_ge(res_done, (s - 1) * SGT + g + 1)
                        columns(x_res[g], s, g, res_in[g])

                load(0, 0)
                load(1, 1)
                load_res(0)
                load(2, 0)
                load_res(1)
                load(3, 1)
                with sp.Fori(1, NSG // 2 - 1) as pair:
                    load_res(pair * 2)
                    load(pair * 2 + 2, 0)
                    load_res(pair * 2 + 1)
                    load(pair * 2 + 3, 1)
                load_res(NSG - 2)
                load_res(NSG - 1)

            @block.tensor
            def _(pe):
                def xtr(u, turn):
                    pe.wait_ge(x_in[u], turn * (16 * NX) + 16 * NX)
                    for k in range(KT):
                        for g in range(SGT):
                            ins = pe.transpose(xT_ps[:, k, g * P:(g + 1) * P], x_nat[u][:, g, k * P:(k + 1) * P],
                                               ident[:])
                    ins.then_inc(xT_done, 1)

                def proj(s, j):
                    if j == 0:
                        pe.wait_ge(xhi_done, s + 1)
                        pe.wait_ge(xlo_done, s + 1)
                    if above_zero(s * (NPROJ // 2) + j // 2):
                        pe.wait_ge(evac_dve if j % 2 else evac_act, s * (NPROJ // 2) + j // 2)
                    bank = proj_ps[j % 2]
                    if j < 8:
                        for h in range(2):
                            c = (2 * j + h) % HC
                            m = 0
                            for k in range(KT):
                                for w, t in ((w_hi, xT_hi), (w_hi, xT_lo), (w_lo, xT_hi)):
                                    ins = pe.matmul(bank[:, h * TOK:(h + 1) * TOK], w[:, j // 4, k, c * P:(c + 1) * P],
                                                    t[:, k, :], start=(m == 0), stop=(m == 5))
                                    m += 1
                    else:
                        g, h = (j - 8) // 2, (j - 8) % 2
                        m = 0
                        for k in range(KT):
                            for t, w in ((xT_hi, w_hi), (xT_hi, w_lo), (xT_lo, w_hi)):
                                ins = pe.matmul(bank[:], t[:, k, g * P:(g + 1) * P], w[:, 2, k, h * 512:(h + 1) * 512],
                                                start=(m == 0), stop=(m == 5))
                                m += 1
                    ins.then_inc(proj_done, 1)

                def scores(T, u, g):
                    if g:
                        pe.wait_ge(s_ident, 1)
                        if above_zero(T):
                            pe.wait_ge(sub_done, T)
                    for n in range(NH):
                        r = (n % 2) * DH
                        for b in range(GB):
                            t0 = g * P + b * L
                            ins = pe.matmul(s_view[b * L:(b + 1) * L, n % 2, n // 2, :], qT[u][r:r + DH, n // 2, t0:t0 + L],
                                            kT[u][r:r + DH, n // 2, t0:t0 + L], start=True, stop=True)
                    ins.then_inc(score_done, 1)

                def context(T, u, g):
                    pe.wait_ge(probT_done, T + 1)
                    if above_zero(T):
                        pe.wait_ge(vlo_done, T)
                    for n in range(NH):
                        r = (n % 2) * DH
                        ins = pe.matmul(vecT_ps[r:r + DH, n // 2, :], v[u][:, g, n * DH:(n + 1) * DH], probT[:, n % 2 * (NH // 2) + n // 2, :],
                                        start=True, stop=True)
                    ins.then_inc(pv_done, 1)

                def project_out(T):
                    pe.wait_ge(vlo_done, T + 1)
                    if above_zero(T):
                        pe.wait_ge(res_done, T)
                    if above_zero(T):
                        pe.wait_ge(yT_done, T)
                    m = 0
                    for c in range(HC):
                        for t, w in ((vecT_hi, wo_hi), (vecT_hi, wo_lo), (vecT_lo, wo_hi)):
                            ins = pe.matmul(o_ps, t[:, c, :], w[:, c, :], start=(m == 0), stop=(m == 3 * HC - 1))
                            m += 1
                    ins.then_inc(o_done, 1)

                def ytr(T):
                    pe.wait_ge(y_done, T + 1)
                    if above_zero(T):
                        pe.wait_ge(yT_done, T)
                    for k in range(KT):
                        ins = pe.transpose(yT_ps[:, k, :], y_nat[:, k * P:(k + 1) * P], ident[:])
                    ins.then_inc(ytr_done, 1)

                def step(s, u, pair, ahead):
                    nxt = s + 1
                    for g in range(SGT):
                        T = s * SGT + g
                        scores(T, u, g)
                        if ahead:
                            for j in range(6 * g, 6 * g + 4):
                                proj(nxt, j)
                        if above_zero(T):
                            project_out(T - 1)
                        if ahead:
                            for j in range(6 * g + 4, 6 * g + 6):
                                proj(nxt, j)
                        context(T, u, g)
                        if above_zero(T):
                            ytr(T - 1)
                    if ahead:
                        pe.wait_ge(evac_act, (s + 2) * (NPROJ // 2))
                        pe.wait_ge(evac_dve, (s + 2) * (NPROJ // 2))
                        pe.wait_ge(sub_done, s * SGT + SGT)
                    if ahead == 2:
                        xtr(u, pair + 1)

                pe.wait_ge(s_ident, 1)
                xtr(0, 0)
                for j in range(NPROJ):
                    proj(0, j)
                pe.wait_ge(evac_act, NPROJ // 2)
                pe.wait_ge(evac_dve, NPROJ // 2)
                xtr(1, 0)
                steps(pe, step)
                project_out(2 * NSG - 1)
                ytr(2 * NSG - 1)

            def evacuated_to(s_parity, j):
                if j < 8:
                    dst = (qT, kT)[j // 4][s_parity]
                    return dst[:, 2 * (j % 4):2 * (j % 4) + 2, :].rearrange("p c t -> p (c t)")
                g, h = (j - 8) // 2, (j - 8) % 2
                return v[s_parity][:, g, h * 512:(h + 1) * 512]

            @block.scalar
            def _(act):
                def xhi(s):
                    act.wait_ge(xT_done, s + 1)
                    if above_zero(s * NPROJ):
                        act.wait_ge(proj_done, s * NPROJ)
                    act.activation(xT_hi[:], xT_ps[:], ACT.Copy).then_inc(xhi_done, 1)

                def evac(s, u, j):
                    act.wait_ge(proj_done, s * NPROJ + (j + 1))
                    act.activation(evacuated_to(u, j), proj_ps[0][:], ACT.Copy).then_inc(evac_act, 1)

                def yT_copy(T):
                    act.wait_ge(ytr_done, T + 1)
                    dst = yT[:].rearrange("p k (i b) -> p k i b", i=L)
                    for k in range(KT):
                        act.activation(dst[:, k, :, bass.ds(T * GB, GB)],
                                       yT_ps[:, k, :].rearrange("p (b i) -> p i b", b=GB),
                                       ACT.Copy).then_inc(yT_done, 1) if k == KT - 1 else \
                            act.activation(dst[:, k, :, bass.ds(T * GB, GB)],
                                           yT_ps[:, k, :].rearrange("p (b i) -> p i b", b=GB), ACT.Copy)

                def step(s, u, pair, ahead):
                    for g in range(SGT):
                        T = s * SGT + g
                        act.wait_ge(sub_done, T + 1)
                        act.activation(prob[:], prob[:], ACT.Exp, scale=SCORE_SCALE).then_inc(exp_done, 1)
                        if ahead:
                            evac(s + 1, 1 - u, 6 * g)
                            evac(s + 1, 1 - u, 6 * g + 2)
                            evac(s + 1, 1 - u, 6 * g + 4)
                        act.wait_ge(pv_done, T + 1)
                        if above_zero(T):
                            act.wait_ge(o_done, T)
                        act.activation(vecT_hi[:], vecT_ps[:], ACT.Copy).then_inc(vhi_done, 1)
                        if above_zero(T):
                            yT_copy(T - 1)
                    if ahead == 2:
                        xhi(s + 2)

                xhi(0)
                for j in range(0, NPROJ, 2):
                    evac(0, 0, j)
                xhi(1)
                steps(act, step)
                yT_copy(2 * NSG - 1)

            @block.vector
            def _(dve):
                def xlo(s):
                    dve.wait_ge(xhi_done, s + 1)
                    dve.tensor_tensor(xT_lo[:], xT_ps[:], f(xT_hi[:]), ALU.subtract).then_inc(xlo_done, 1)

                def evac(s, u, j):
                    dve.wait_ge(proj_done, s * NPROJ + (j + 1))
                    dve.tensor_copy(evacuated_to(u, j), proj_ps[1][:]).then_inc(evac_dve, 1)

                def norm(s, T, g):
                    dve.wait_ge(res_in[g], (s + 1) * (16 * GB))
                    dve.wait_ge(o_done, T + 1)
                    dve.tensor_tensor(res[:], o_ps, x_res[g][:], ALU.add).then_inc(res_done, 1)
                    dve.wait_ge(res_done, T + 1)
                    dve.bn_stats(stats[:], res[:]).then_inc(st_done, 1)
                    dve.wait_ge(s_ident, 1)
                    dve.wait_ge(st_done, T + 1)
                    dve.bn_aggr(mv[:], stats[:]).then_inc(mv_done, 1)
                    dve.wait_ge(mv_done, T + 1)
                    dve.tensor_scalar(veps[:], mv[:, 1:2], EPS, None, ALU.add).then_inc(eps_done, 1)

                def norm_out(T):
                    dve.wait_ge(rstd_done, T + 1)
                    if above_zero(T):
                        dve.wait_ge(ytr_done, T)
                    dve.tensor_scalar(y_nat[:], res[:], mv[:, 0:1], rstd[:], ALU.subtract, ALU.mult).then_inc(y_done, 1)

                def step(s, u, pair, ahead):
                    for g in range(SGT):
                        T = s * SGT + g
                        dve.wait_ge(score_done, T + 1)
                        dve.tensor_reduce(rowmax[:].rearrange("p (r n) -> p r n", r=2), s_view, AX.X, ALU.max).then_inc(max_done, 1)
                        dve.wait_ge(max_done, T + 1)
                        dve.tensor_tensor(prob4, s_view, rowmax[:].rearrange("p (r n) -> p r n", r=2).unsqueeze(3)
                                          .broadcast_to([P, 2, NH // 2, L]), ALU.subtract).then_inc(sub_done, 1)
                        if ahead:
                            evac(s + 1, 1 - u, 6 * g + 1)
                        dve.wait_ge(exp_done, T + 1)
                        dve.tensor_reduce(rowsum[:], prob[:], AX.X, ALU.add).then_inc(sum_done, 1)
                        dve.wait_ge(sum_done, T + 1)
                        dve.reciprocal(rowinv[:], rowsum[:]).then_inc(inv_done, 1)
                        if ahead:
                            evac(s + 1, 1 - u, 6 * g + 3)
                        dve.wait_ge(prob_done, T + 1)
                        if above_zero(T):
                            dve.wait_ge(pv_done, T)
                        for b in range(GB):
                            ins = dve.transpose(probT[b * L:(b + 1) * L, :, b * L:(b + 1) * L],
                                                prob[b * L:(b + 1) * L, :, :])
                        ins.then_inc(probT_done, 1)
                        if above_zero(T):
                            norm(s - (1 - g), T - 1, 1 - g)
                            norm_out(T - 1)
                        if ahead:
                            evac(s + 1, 1 - u, 6 * g + 5)
                        dve.wait_ge(vhi_done, T + 1)
                        dve.tensor_tensor(vecT_lo[:], vecT_ps[:], f(vecT_hi[:]), ALU.subtract).then_inc(vlo_done, 1)
                    if ahead == 2:
                        xlo(s + 2)

                xlo(0)
                for j in range(1, NPROJ, 2):
                    evac(0, 0, j)
                xlo(1)
                steps(dve, step)
                norm(NSG - 1, 2 * NSG - 1, 1)
                norm_out(2 * NSG - 1)

            @block.gpsimd
            def _(pool):
                def rstd_of(T):
                    pool.wait_ge(eps_done, T + 1)
                    pool.tensor_tensor(rstd[:], veps[:], neg_half[:, 0:1], ALU.pow).then_inc(rstd_done, 1)

                def step(s, u, pair, ahead):
                    for g in range(SGT):
                        T = s * SGT + g
                        pool.wait_ge(inv_done, T + 1)
                        pool.tensor_tensor(prob[:], prob[:], rowinv[:].unsqueeze(2).broadcast_to([P, NH, L]),
                                           ALU.mult).then_inc(prob_done, 1)
                        if above_zero(T):
                            rstd_of(T - 1)

                steps(pool, step)
                rstd_of(2 * NSG - 1)


def cross_and_tree(nc, sem, ctx_in, w_cq, b_cq, w_c, b_c, w_q, b_q, WlT, b_l, fWq, routersT, leafT, WoutT, Wout_b,
                   yT, ident, neg_half, s_ident, out):
    NGATE = routersT.shape[1]
    CT = NB // P
    with ExitStack() as ctx:
        def sb(name, shape, dt=F32):
            return ctx.enter_context(nc.sbuf_tensor(name, shape, dt))

        def ps(name, shape):
            return ctx.enter_context(nc.psum_tensor(name, shape, F32))

        def halves(name, shape, n):
            return [(sb(f"{name}_hi{u}", shape, F32R), sb(f"{name}_lo{u}", shape, F32R)) for u in range(n)]

        wl_raw = sb("wl_raw", [P, 4, KT, D])
        w1_id = sb("w1_id", [P, KT, D])
        [(w2_hi, w2_lo)] = halves("w2", [P, KT, D], 1)
        [(w3_hi, w3_lo)] = halves("w3", [P, KT, D], 1)
        fwq = sb("fwq", [P, KT, D])
        routers = sb("routers", [P, KT, LEAVES])
        leaf_v = sb("leaf_v", [P, KT, LEAVES])
        wout = sb("wout", [P, KT, D])
        gate_w = sb("gate_w", [P, KT, LEAVES])
        leaf_w = sb("leaf_w", [P, KT, D])
        [(gate_hi, gate_lo)] = halves("gate", [P, KT, LEAVES], 1)
        [(leafw_hi, leafw_lo)] = halves("leafw", [P, KT, D], 1)
        vec3 = sb("vec3", [P, 3, KT])
        consts = sb("consts", [P, 3])
        const = sb("const", [P, 1])
        wq_rows = sb("wq_rows", [P, KT, P])
        ones = sb("ones", [P, P])
        ones_r = sb("ones_r", [P, P], F32R)
        bias_raw = sb("bias_raw", [1, 2, D])
        bias_hi = sb("bias_hi", [1, 2, D], F32R)
        bias_lo = sb("bias_lo", [1, 2, D], F32R)

        q_nat = [sb(f"q_nat{u}", [NQ, D]) for u in range(2)]
        qT = sb("cqT", [P, KT, NQ])
        g_mat = sb("g_mat", [P, KT, NQ])
        c = sb("c", [P, KT, NB])
        c_r = halves("c", [P, KT, NB], 2)
        u_r = halves("u", [P, KT, NB], 2)
        w_r = halves("w", [P, KT, NB], 2)
        we_r = halves("we", [P, KT, D], 2)
        w32 = sb("w32", [P, KT, NB])
        we32 = sb("we32", [P, KT, D])
        s_sb = sb("s_sb", [P, CT, NQ])
        a_sb = sb("a_sb", [P, CT, NQ])
        aT = sb("aT", [NQ, NB])
        smax = sb("smax", [P, CT])
        ssum = sb("ssum", [P, CT])
        sinv = sb("sinv", [P, CT])
        diag = sb("diag", [P, CT, P])
        neg_m = sb("neg_m", [P, 1])
        eb = sb("eb", [P, NB])
        ebsum = sb("ebsum", [P, 1])
        ebinv = sb("ebinv", [P, 1])
        scratch = sb("scratch", [P, KT, NB])
        q2_raw = sb("q2_raw", [P, KT])
        q2 = sb("q2", [P, KT])
        y2 = [sb(f"y2_{u}", [P, CT, D]) for u in range(2)]
        [(y2T_hi, y2T_lo)] = halves("y2T", [P, KT, NB], 1)
        th = sb("th", [P, CT, LEAVES])
        lv = [sb(f"lv{u}", [P, CT, LEAVES // 2]) for u in range(2)]
        leaf = sb("leaf", [P, CT, LEAVES])
        [(lT_hi, lT_lo)] = halves("lT", [P, KT, NB], 1)
        r3 = sb("r3", [P, CT, D])
        y3 = [sb(f"y3_{u}", [P, CT, D]) for u in range(2)]
        st = [sb(f"st{n}", [P, CT, 6]) for n in (2, 3)]
        mv = [sb(f"mv{n}", [P, CT, 2]) for n in (2, 3)]
        veps = [sb(f"veps{n}", [P, CT]) for n in (2, 3)]
        rstd = [sb(f"rstd{n}", [P, CT]) for n in (2, 3)]

        so_ps = ps("so_ps", [P, 512])
        lq_ps = ps("lq_ps", [P, 512])
        z_ps = ps("z_ps", [P, CT, D])
        bc_ps = ps("bc_ps", [P, 512])
        aT_ps = ps("aT_ps", [P, 512])
        c2q_ps = ps("c2q_ps", [P, KT, NB])
        y2T_ps = ps("y2T_ps", [P, KT, NB])
        gate_ps = ps("gate_ps", [P, CT, LEAVES])
        s_ps = so_ps[:, 0:CT * NQ].rearrange("p (c q) -> p c q", c=CT)
        out_ps = so_ps[:].rearrange("p (c d) -> p c d", c=CT)
        lT_ps = lq_ps[:].rearrange("p (k t) -> p k t", k=KT)
        qT_ps = lq_ps[:, 0:KT * NQ].rearrange("p (k q) -> p k q", k=KT)

        ld, fused, setup = sem("c_loaded"), sem("c_fused"), sem("c_setup")
        setup_v = [0]
        with nc.allow_non_contiguous_dma("small vectors"), nc.Block() as block:
            @block.sync
            def _(sp):
                sp.dma_start(wl_raw[:], WlT.rearrange("(f k p) e -> p f k e", f=4, p=P)).then_inc(ld, 16)
                sp.dma_start(fwq[:], fWq.rearrange("(k p) d -> p k d", p=P)).then_inc(ld, 16)
                sp.dma_start(routers[:, :, 0:NGATE], routersT.rearrange("(k p) m -> p k m", p=P)).then_inc(ld, 16)
                sp.dma_start(leaf_v[:], leafT.rearrange("(k p) m -> p k m", p=P)).then_inc(ld, 16)
                sp.dma_start(wout[:], WoutT.rearrange("(k p) e -> p k e", p=P)).then_inc(ld, 16)
                for n, w in enumerate((w_cq, w_c, w_q)):
                    sp.dma_start(vec3[:, n, :], w.rearrange("(k p) -> p k", p=P)).then_inc(ld, 16)
                for n, b in enumerate((b_cq, b_c, b_q)):
                    sp.dma_start(consts[:, n:n + 1], b.partition_broadcast(P)).then_inc(ld, 16)
                sp.dma_start(bias_raw[:, 0, :], b_l.rearrange("(a e) -> a e", a=1)).then_inc(ld, 16)
                sp.dma_start(bias_raw[:, 1, :], Wout_b.rearrange("(a e) -> a e", a=1)).then_inc(ld, 16)

            @block.tensor
            def _(pe):
                pe.wait_ge(ld, 16 * 13)
                pe.wait_ge(setup, 1)
                for k in range(KT):
                    for e in range(KT):
                        pe.matmul(z_ps[:, k, :], fwq[:, e, k * P:(k + 1) * P], routers[:, e, :], start=(e == 0),
                                  stop=(e == KT - 1))
                for k in range(KT):
                    for e in range(KT):
                        ins = pe.matmul(c2q_ps[:, k, :], leaf_v[:, e, k * P:(k + 1) * P], wout[:, e, :],
                                        start=(e == 0), stop=(e == KT - 1))
                ins.then_inc(fused, 1)

            @block.vector
            def _(dve):
                def chain(ins):
                    setup_v[0] += 1
                    ins.then_inc(setup, 1)
                    dve.wait_ge(setup, setup_v[0])

                chain(dve.memset(routers[:, :, NGATE:LEAVES], 0.0))
                dve.wait_ge(ld, 16 * 13)
                chain(dve.memset(ones[:], 1.0))
                chain(dve.tensor_copy(ones_r[:], ones[:]))
                for k in range(KT):
                    chain(dve.tensor_scalar(wq_rows[:, k, :], ones[:], vec3[:, 2, k:k + 1], None, ALU.mult))
                chain(dve.tensor_tensor(const[:], consts[:, 0:1], consts[:, 1:2], ALU.add))
                chain(dve.tensor_tensor(const[:], const[:], consts[:, 2:3], ALU.add))
                chain(dve.tensor_copy(w1_id[:], wl_raw[:, 0]))
                for k in range(KT):
                    part = w1_id[:, k, k * P:(k + 1) * P]
                    chain(dve.tensor_tensor(part, part, ident[:], ALU.add))
                for src, hi, lo in ((wl_raw[:, 1], w2_hi, w2_lo), (wl_raw[:, 2], w3_hi, w3_lo),
                                    (bias_raw[:], bias_hi, bias_lo)):
                    chain(dve.tensor_copy(hi[:], src))
                    chain(dve.tensor_tensor(lo[:], src, f(hi[:]), ALU.subtract))
                dve.wait_ge(fused, 1)
                chain(dve.tensor_copy(gate_w[:], z_ps[:]))
                chain(dve.tensor_scalar(leaf_w[:], c2q_ps[:], 2.0 ** -DEPTH, None, ALU.mult))
                for src, hi, lo in ((gate_w, gate_hi, gate_lo), (leaf_w, leafw_hi, leafw_lo)):
                    chain(dve.tensor_copy(hi[:], src[:]))
                    chain(dve.tensor_tensor(lo[:], src[:], f(hi[:]), ALU.subtract))

        q_in = [sem(f"q_in{u}") for u in range(2)]
        gate_done = sem("gate_done")
        scores_done = sem("scores_done")
        z_done = sem("z_done")
        maxrow_done = sem("maxrow_done")
        aTr_done = sem("aTr_done")
        leafTr_done = sem("leafTr_done")
        c2q_done = sem("c2q_done")
        y2Tr_done = sem("y2Tr_done")
        qTr_done = sem("qTr_done")
        tree_done = sem("tree_done")
        tanh_done = sem("tanh_done")
        a_exp_done = sem("a_exp_done")
        b_exp_done = sem("b_exp_done")
        aT_copied = sem("aT_copied")
        lT_hi_done = sem("lT_hi_done")
        we_hi_done = sem("we_hi_done")
        u_hi_done = sem("u_hi_done")
        w_hi_done = sem("w_hi_done")
        y2T_hi_done = sem("y2T_hi_done")
        g_mat_done = sem("g_mat_done")
        c_hi_done = sem("c_hi_done")
        s_copied = sem("s_copied")
        smax_done = sem("smax_done")
        s_sub_done = sem("s_sub_done")
        diag_done = sem("diag_done")
        ssum_done = sem("ssum_done")
        sinv_done = sem("sinv_done")
        a_done = sem("a_done")
        z_stats_done = sem("z_stats_done")
        z_mean_done = sem("z_mean_done")
        z_var_done = sem("z_var_done")
        y2_done = sem("y2_done")
        neg_m_done = sem("neg_m_done")
        q2_sum_done = sem("q2_sum_done")
        eb_inv_done = sem("eb_inv_done")
        q2_done = sem("q2_done")
        we_done = sem("we_done")
        u_lo_done = sem("u_lo_done")
        w_done = sem("w_done")
        lT_lo_done = sem("lT_lo_done")
        y2T_lo_done = sem("y2T_lo_done")
        qT_copied = sem("qT_copied")
        c_copied = sem("c_copied")
        c_lo_done = sem("c_lo_done")
        res3_done = sem("res3_done")
        r3_stats_done = sem("r3_stats_done")
        r3_mean_done = sem("r3_mean_done")
        r3_var_done = sem("r3_var_done")
        y3_done = sem("y3_done")
        leaves_done = sem("leaves_done")
        rstd2_done = sem("rstd2_done")
        we_lo_done = sem("we_lo_done")
        w_lo_done = sem("w_lo_done")
        rstd3_done = sem("rstd3_done")
        level_done = sem("level_done")
        y_out = [sem(f"y_out{u}") for u in range(2)]
        NLV = 2 * DEPTH - 1

        def steps(eng, step):
            for t in range(-2, 4):
                step(t, t % 2, t // 2)
            with eng.Fori(2, L // 2 - 1) as pair:
                step(pair * 2, 0, pair)
                step(pair * 2 + 1, 1, pair)
            for t in range(L - 2, L + 2):
                step(t, t % 2, t // 2)

        with nc.Block() as block:
            @block.sync
            def _(sp):
                def load(b, u):
                    if begun(b - 2):
                        sp.wait_ge(c2q_done, count(b - 2))
                    sp.dma_start(q_nat[u][:], ctx_in[bass.ds(b, 1), :, :].rearrange("a q d -> (a q) d"))\
                        .then_inc(q_in[u], 16)

                def store(b, u):
                    sp.wait_ge(y3_done, count(b))
                    for ct in range(CT):
                        sp.dma_start(out[bass.ds(b, 1), ct * P:(ct + 1) * P, :].rearrange("a c d -> (a c) d"),
                                     y3[u][:, ct, :]).then_inc(y_out[u], 16)

                def step(t, u, pair):
                    if live(t + 3):
                        load(t + 3, 1 - u)
                    if live(t - 1):
                        store(t - 1, 1 - u)

                load(0, 0)
                for t in range(-2, 4):
                    step(t, t % 2, t // 2)
                with sp.Fori(2, L // 2 - 2) as pair:
                    step(pair * 2, 0, pair)
                    step(pair * 2 + 1, 1, pair)
                for t in range(L - 4, L + 2):
                    step(t, t % 2, t // 2)
                for u in range(2):
                    sp.wait_ge(y_out[u], 16 * CT * (L // 2))

            @block.tensor
            def _(pe):
                def three(dst, lt, rt, first, last):
                    m = 0
                    for k in range(KT):
                        for a, b in ((0, 0), (0, 1), (1, 0)):
                            ins = pe.matmul(dst, lt(a, k), rt(b, k), start=(first and m == 0),
                                            stop=(last and m == 3 * KT - 1))
                            m += 1
                    return ins

                def add_bias(dst, n):
                    pe.matmul(dst, ones_r[0:1, :], bias_hi[:, n, :], start=False, stop=False)
                    return pe.matmul(dst, ones_r[0:1, :], bias_lo[:, n, :], start=False, stop=True)

                def step(t, u, pair):
                    v_ = 1 - u
                    if live(t - 1):
                        pe.wait_ge(y2T_hi_done, count(t - 1))
                        pe.wait_ge(y2T_lo_done, count(t - 1))
                        if begun(t - 2):
                            pe.wait_ge(tanh_done, count(t - 2))
                        for ct in range(CT):
                            ins = three(gate_ps[:, ct, :], lambda a, k: (y2T_hi, y2T_lo)[a][:, k, ct * P:(ct + 1) * P],
                                        lambda b, k: (gate_hi, gate_lo)[b][:, k, :], True, True)
                        ins.then_inc(gate_done, 1)
                    if live(t + 1):
                        pe.wait_ge(c_copied, count(t + 1))
                        pe.wait_ge(g_mat_done, count(t + 1))
                        pe.wait_ge(qT_copied, count(t + 1))
                        if begun(t):
                            pe.wait_ge(s_copied, count(t))
                        if begun(t - 2):
                            pe.wait_ge(res3_done, count(t - 2))
                        for ct in range(CT):
                            for k in range(KT):
                                pe.matmul(s_ps[:, ct, :], c[:, k, ct * P:(ct + 1) * P], g_mat[:, k, :], start=(k == 0),
                                          stop=False)
                            for k in range(KT):
                                ins = pe.matmul(s_ps[:, ct, :], wq_rows[:, k, :], qT[:, k, :], start=False,
                                                stop=(k == KT - 1))
                        ins.then_inc(scores_done, 1)
                    if live(t):
                        pe.wait_ge(c_hi_done, count(t))
                        pe.wait_ge(c_lo_done, count(t))
                        pe.wait_ge(u_hi_done, count(t))
                        pe.wait_ge(u_lo_done, count(t))
                        pe.wait_ge(w_hi_done, count(t))
                        pe.wait_ge(w_lo_done, count(t))
                        pe.wait_ge(we_hi_done, count(t))
                        pe.wait_ge(we_lo_done, count(t))
                        if begun(t - 1):
                            pe.wait_ge(z_stats_done, count(t - 1))
                        if begun(t - 1):
                            pe.wait_ge(y2_done, count(t - 1))
                        for ct in range(CT):
                            sl = slice(ct * P, (ct + 1) * P)
                            three(z_ps[:, ct, :], lambda a, k: c_r[u][a][:, k, sl], lambda b, k: we_r[u][b][:, k, :],
                                  True, False)
                            three(z_ps[:, ct, :], lambda a, k: u_r[u][a][:, k, sl],
                                  lambda b, k: (w2_hi, w2_lo)[b][:, k, :], False, False)
                            three(z_ps[:, ct, :], lambda a, k: w_r[u][a][:, k, sl],
                                  lambda b, k: (w3_hi, w3_lo)[b][:, k, :], False, False)
                            ins = add_bias(z_ps[:, ct, :], 0)
                        ins.then_inc(z_done, 1)
                    if live(t + 1):
                        pe.wait_ge(diag_done, count(t + 1))
                        if begun(t):
                            pe.wait_ge(b_exp_done, count(t))
                        pe.matmul(bc_ps[:, 0:NB], ones[:], diag[:].rearrange("p c t -> p (c t)"), start=True,
                                  stop=True).then_inc(maxrow_done, 1)
                        pe.wait_ge(a_done, count(t + 1))
                        if begun(t):
                            pe.wait_ge(aT_copied, count(t))
                        for ct in range(CT):
                            ins = pe.transpose(aT_ps[0:NQ, ct * P:(ct + 1) * P], a_sb[:, ct, :], ident[:])
                        ins.then_inc(aTr_done, 1)
                    if live(t - 1):
                        pe.wait_ge(leaves_done, count(t - 1))
                        pe.wait_ge(g_mat_done, count(t + 1))
                        pe.wait_ge(qT_copied, count(t + 1))
                        for k in range(KT):
                            for ct in range(CT):
                                ins = pe.transpose(lT_ps[:, k, ct * P:(ct + 1) * P], leaf[:, ct, k * P:(k + 1) * P],
                                                   ident[:])
                        ins.then_inc(leafTr_done, 1)
                    if live(t + 1):
                        pe.wait_ge(aT_copied, count(t + 1))
                        if begun(t):
                            pe.wait_ge(u_lo_done, count(t))
                        if begun(t):
                            pe.wait_ge(w_done, count(t))
                        for k in range(KT):
                            ins = pe.matmul(c2q_ps[:, k, :], q_nat[v_][:, k * P:(k + 1) * P], aT[:], start=True, stop=True)
                        ins.then_inc(c2q_done, 1)
                    if live(t):
                        pe.wait_ge(y2_done, count(t))
                        if begun(t - 1):
                            pe.wait_ge(y2T_lo_done, count(t - 1))
                        for k in range(KT):
                            for ct in range(CT):
                                ins = pe.transpose(y2T_ps[:, k, ct * P:(ct + 1) * P], y2[u][:, ct, k * P:(k + 1) * P],
                                                   ident[:])
                        ins.then_inc(y2Tr_done, 1)
                    if live(t + 2):
                        pe.wait_ge(q_in[u], pair * 16 + 32)
                        if begun(t - 1):
                            pe.wait_ge(lT_lo_done, count(t - 1))
                        for k in range(KT):
                            ins = pe.transpose(qT_ps[:, k, :], q_nat[u][:, k * P:(k + 1) * P], ident[0:NQ, 0:NQ])
                        ins.then_inc(qTr_done, 1)
                    if live(t - 1):
                        pe.wait_ge(lT_hi_done, count(t - 1))
                        pe.wait_ge(lT_lo_done, count(t - 1))
                        pe.wait_ge(s_copied, count(t + 1))
                        if begun(t - 2):
                            pe.wait_ge(res3_done, count(t - 2))
                        for ct in range(CT):
                            three(out_ps[:, ct, :], lambda a, k: (lT_hi, lT_lo)[a][:, k, ct * P:(ct + 1) * P],
                                  lambda b, k: (leafw_hi, leafw_lo)[b][:, k, :], True, False)
                            ins = add_bias(out_ps[:, ct, :], 1)
                        ins.then_inc(tree_done, 1)

                steps(pe, step)

            @block.scalar
            def _(act):
                def step(t, u, pair):
                    v_ = 1 - u
                    if live(t - 1):
                        act.wait_ge(gate_done, count(t - 1))
                        if begun(t - 2):
                            act.wait_ge(leaves_done, count(t - 2))
                        act.activation(th[:], gate_ps[:], ACT.Tanh, scale=0.5).then_inc(tanh_done, 1)
                    if live(t + 1):
                        act.wait_ge(s_sub_done, count(t + 1))
                        if begun(t):
                            act.wait_ge(a_done, count(t))
                        act.activation(a_sb[:], s_sb[:], ACT.Exp).then_inc(a_exp_done, 1)
                        act.wait_ge(c_copied, count(t + 1))
                        if begun(t - 1):
                            act.wait_ge(z_done, count(t - 1))
                        act.activation(c_r[v_][0][:], c[:], ACT.Copy).then_inc(c_hi_done, 1)
                        act.wait_ge(neg_m_done, count(t + 1))
                        if begun(t):
                            act.wait_ge(q2_sum_done, count(t))
                        act.activation(eb[:], bc_ps[:, 0:NB], ACT.Exp, bias=neg_m[:], accum_out=ebsum[:])\
                            .then_inc(b_exp_done, 1)
                        act.wait_ge(aTr_done, count(t + 1))
                        if begun(t):
                            act.wait_ge(c2q_done, count(t))
                        act.activation(aT[:], aT_ps[0:NQ, 0:NB], ACT.Copy).then_inc(aT_copied, 1)
                    if live(t - 1):
                        act.wait_ge(leafTr_done, count(t - 1))
                        if begun(t - 2):
                            act.wait_ge(tree_done, count(t - 2))
                        act.activation(lT_hi[:], lT_ps, ACT.Copy).then_inc(lT_hi_done, 1)
                    if live(t + 1):
                        act.wait_ge(c2q_done, count(t + 1))
                        act.activation(u_r[v_][0][:], c2q_ps[:], ACT.Copy).then_inc(u_hi_done, 1)
                        act.wait_ge(we_done, count(t + 1))
                        act.activation(we_r[v_][0][:], we32[:], ACT.Copy).then_inc(we_hi_done, 1)
                        act.wait_ge(w_done, count(t + 1))
                        act.activation(w_r[v_][0][:], w32[:], ACT.Copy).then_inc(w_hi_done, 1)
                    if live(t):
                        act.wait_ge(y2Tr_done, count(t))
                        if begun(t - 1):
                            act.wait_ge(gate_done, count(t - 1))
                        act.activation(y2T_hi[:], y2T_ps[:], ACT.Copy).then_inc(y2T_hi_done, 1)
                    if live(t + 2):
                        act.wait_ge(qTr_done, count(t + 2))
                        if begun(t + 1):
                            act.wait_ge(scores_done, count(t + 1))
                        for k in range(KT):
                            ins = act.activation(g_mat[:, k, :], qT_ps[:, k, :], ACT.Identity, scale=vec3[:, 0, k:k + 1],
                                                 bias=vec3[:, 1, k:k + 1])
                        ins.then_inc(g_mat_done, 1)

                steps(act, step)

            @block.vector
            def _(dve):
                def stats(n, b, src, stats_done, mean_done, var_done):
                    for ct in range(CT):
                        ins = dve.bn_stats(st[n][:, ct, :], src(ct))
                    ins.then_inc(stats_done, 1)
                    dve.wait_ge(s_ident, 1)
                    dve.wait_ge(stats_done, count(b))
                    for ct in range(CT):
                        ins = dve.bn_aggr(mv[n][:, ct, :], st[n][:, ct, :])
                    ins.then_inc(mean_done, 1)
                    dve.wait_ge(mean_done, count(b))
                    dve.tensor_scalar(veps[n][:], mv[n][:, :, 1], EPS, None, ALU.add).then_inc(var_done, 1)

                def leaves(b):
                    base = b * NLV
                    k = 0
                    dve.wait_ge(tanh_done, count(b))
                    dve.tensor_scalar(lv[0][:, :, 0:1], th[:, :, 0:1], -1.0, 1.0, ALU.mult, ALU.add).then_inc(level_done, 1)
                    dve.tensor_scalar(lv[0][:, :, 1:2], th[:, :, 0:1], 1.0, None, ALU.add).then_inc(level_done, 1)
                    k += 2
                    src = lv[0]
                    for level in range(1, DEPTH):
                        n = 2 ** level
                        last = level == DEPTH - 1
                        if last:
                            if begun(b - 1):
                                dve.wait_ge(leafTr_done, count(b - 1))
                        dst = leaf if last else lv[level % 2]
                        kids = dst[:, :, 0:2 * n].rearrange("p c (m two) -> p c m two", two=2)
                        dve.wait_ge(level_done, base + k)
                        dve.scalar_tensor_tensor(kids[:, :, :, 1], th[:, :, n - 1:2 * n - 1], 1.0, src[:, :, 0:n],
                                                 ALU.add, ALU.mult).then_inc(level_done, 1)
                        k += 1
                        dve.wait_ge(level_done, base + k)
                        ins = dve.scalar_tensor_tensor(kids[:, :, :, 0], src[:, :, 0:n], 2.0, kids[:, :, :, 1],
                                                       ALU.mult, ALU.subtract)
                        k += 1
                        ins.then_inc(leaves_done if last else level_done, 1)
                        src = dst

                def step(t, u, pair):
                    v_ = 1 - u
                    if live(t + 1):
                        dve.wait_ge(scores_done, count(t + 1))
                        if begun(t):
                            dve.wait_ge(a_exp_done, count(t))
                        dve.tensor_scalar(s_sb[:], s_ps, const[:], None, ALU.add).then_inc(s_copied, 1)
                        dve.wait_ge(s_copied, count(t + 1))
                        dve.tensor_reduce(smax[:], s_sb[:], AX.X, ALU.max).then_inc(smax_done, 1)
                        dve.wait_ge(smax_done, count(t + 1))
                        dve.tensor_tensor(s_sb[:], s_sb[:], smax[:].unsqueeze(2).broadcast_to([P, CT, NQ]),
                                          ALU.subtract).then_inc(s_sub_done, 1)
                        if begun(t):
                            dve.wait_ge(maxrow_done, count(t))
                        for ct in range(CT):
                            ins = dve.tensor_scalar(diag[:, ct, :], ident[:], smax[:, ct:ct + 1], None, ALU.mult)
                        ins.then_inc(diag_done, 1)
                    if live(t - 1):
                        leaves(t - 1)
                    if live(t + 1):
                        dve.wait_ge(a_exp_done, count(t + 1))
                        dve.tensor_reduce(ssum[:], a_sb[:], AX.X, ALU.add).then_inc(ssum_done, 1)
                        dve.wait_ge(ssum_done, count(t + 1))
                        dve.reciprocal(sinv[:], ssum[:]).then_inc(sinv_done, 1)
                        dve.wait_ge(sinv_done, count(t + 1))
                        dve.tensor_tensor(a_sb[:], a_sb[:], sinv[:].unsqueeze(2).broadcast_to([P, CT, NQ]),
                                          ALU.mult).then_inc(a_done, 1)
                        dve.wait_ge(c_hi_done, count(t + 1))
                        dve.tensor_tensor(c_r[v_][1][:], c[:], f(c_r[v_][0][:]), ALU.subtract).then_inc(c_lo_done, 1)
                        dve.wait_ge(maxrow_done, count(t + 1))
                        dve.tensor_reduce(neg_m[:], bc_ps[:, 0:NB], AX.X, ALU.max, negate=True).then_inc(neg_m_done, 1)
                    if live(t):
                        dve.wait_ge(z_done, count(t))
                        stats(0, t, lambda ct: z_ps[:, ct, :], z_stats_done, z_mean_done, z_var_done)
                    if live(t + 1):
                        dve.wait_ge(b_exp_done, count(t + 1))
                        for k in range(KT):
                            ins = dve.tensor_tensor_reduce(scratch[:, k, :], c[:, k, :], eb[:], 1.0, 0.0, ALU.mult, ALU.add,
                                                           q2_raw[:, k:k + 1])
                        ins.then_inc(q2_sum_done, 1)
                        dve.reciprocal(ebinv[:], ebsum[:]).then_inc(eb_inv_done, 1)
                        dve.wait_ge(eb_inv_done, count(t + 1))
                        dve.wait_ge(q2_sum_done, count(t + 1))
                        dve.tensor_scalar(q2[:], q2_raw[:], ebinv[:], None, ALU.mult).then_inc(q2_done, 1)
                    if live(t):
                        dve.wait_ge(rstd2_done, count(t))
                        if begun(t - 2):
                            dve.wait_ge(y2Tr_done, count(t - 2))
                        if begun(t - 2):
                            dve.wait_ge(res3_done, count(t - 2))
                        for ct in range(CT):
                            ins = dve.tensor_scalar(y2[u][:, ct, :], z_ps[:, ct, :], mv[0][:, ct, 0:1],
                                                    rstd[0][:, ct:ct + 1], ALU.subtract, ALU.mult)
                        ins.then_inc(y2_done, 1)
                    if live(t + 1):
                        dve.wait_ge(q2_done, count(t + 1))
                        if begun(t):
                            dve.wait_ge(we_lo_done, count(t))
                        if begun(t):
                            dve.wait_ge(we_hi_done, count(t))
                        for k in range(KT):
                            ins = dve.scalar_tensor_tensor(we32[:, k, :], wl_raw[:, 3, k, :], q2[:, k:k + 1],
                                                           w1_id[:, k, :], ALU.mult, ALU.add)
                        ins.then_inc(we_done, 1)
                        dve.wait_ge(c2q_done, count(t + 1))
                        if begun(t):
                            dve.wait_ge(w_lo_done, count(t))
                        if begun(t):
                            dve.wait_ge(w_hi_done, count(t))
                        dve.wait_ge(u_hi_done, count(t + 1))
                        dve.tensor_tensor(w32[:], c2q_ps[:], c[:], ALU.mult).then_inc(w_done, 1)
                        dve.tensor_tensor(u_r[v_][1][:], c2q_ps[:], f(u_r[v_][0][:]), ALU.subtract).then_inc(u_lo_done, 1)
                    if live(t - 1):
                        dve.wait_ge(lT_hi_done, count(t - 1))
                        dve.tensor_tensor(lT_lo[:], lT_ps, f(lT_hi[:]), ALU.subtract).then_inc(lT_lo_done, 1)
                    if live(t):
                        dve.wait_ge(y2T_hi_done, count(t))
                        dve.tensor_tensor(y2T_lo[:], y2T_ps[:], f(y2T_hi[:]), ALU.subtract).then_inc(y2T_lo_done, 1)
                    if live(t + 2):
                        dve.wait_ge(g_mat_done, count(t + 2))
                        dve.tensor_copy(qT[:], qT_ps).then_inc(qT_copied, 1)
                        if begun(t + 1):
                            dve.wait_ge(scores_done, count(t + 1))
                        if begun(t + 1):
                            dve.wait_ge(c_hi_done, count(t + 1))
                        dve.tensor_copy(c[:], yT[:, :, bass.ds((t + 2) * NB, NB)]).then_inc(c_copied, 1)
                    if live(t - 1):
                        dve.wait_ge(tree_done, count(t - 1))
                        dve.tensor_tensor(r3[:], out_ps, y2[v_][:], ALU.add).then_inc(res3_done, 1)
                        dve.wait_ge(res3_done, count(t - 1))
                        stats(1, t - 1, lambda ct: r3[:, ct, :], r3_stats_done, r3_mean_done, r3_var_done)
                        dve.wait_ge(rstd3_done, count(t - 1))
                        if above_zero(pair - (1 - u)):
                            dve.wait_ge(y_out[v_], (pair - (1 - u)) * (16 * CT))
                        for ct in range(CT):
                            ins = dve.tensor_scalar(y3[v_][:, ct, :], r3[:, ct, :], mv[1][:, ct, 0:1],
                                                    rstd[1][:, ct:ct + 1], ALU.subtract, ALU.mult)
                        ins.then_inc(y3_done, 1)

                steps(dve, step)

            @block.gpsimd
            def _(pool):
                def step(t, u, pair):
                    v_ = 1 - u
                    if live(t):
                        pool.wait_ge(z_var_done, count(t))
                        pool.tensor_tensor(rstd[0][:], veps[0][:], neg_half[:], ALU.pow).then_inc(rstd2_done, 1)
                    if live(t + 1):
                        pool.wait_ge(we_hi_done, count(t + 1))
                        pool.tensor_tensor(we_r[v_][1][:], we32[:], f(we_r[v_][0][:]), ALU.subtract)\
                            .then_inc(we_lo_done, 1)
                        pool.wait_ge(w_hi_done, count(t + 1))
                        pool.tensor_tensor(w_r[v_][1][:], w32[:], f(w_r[v_][0][:]), ALU.subtract).then_inc(w_lo_done, 1)
                    if live(t - 1):
                        pool.wait_ge(r3_var_done, count(t - 1))
                        pool.tensor_tensor(rstd[1][:], veps[1][:], neg_half[:], ALU.pow).then_inc(rstd3_done, 1)

                steps(pool, step)


_INS = ["x", "ctx_1024", "L0_attn_Wq", "L0_attn_Wkv", "L0_attn_Wo", "L0_xattn_w_cq", "L0_xattn_b_cq", "L0_xattn_w_c",
        "L0_xattn_b_c", "L0_xattn_w_q", "L0_xattn_b_q", "L0_xattn_W_l", "L0_xattn_b_l", "L0_ffn_Wq",
        "L0_ffn_routers", "L0_ffn_leaf_values", "L0_ffn_Wout_w", "L0_ffn_Wout_b"]
_TRANSPOSED = ("L0_xattn_W_l", "L0_ffn_routers", "L0_ffn_leaf_values", "L0_ffn_Wout_w")


def kernel(**inputs):
    import numpy as _np
    import concourse.bacc as _bacc
    from concourse import mybir as _mybir
    from concourse.bass_utils import run_bass_kernel_spmd as _run

    nc = _bacc.Bacc("TRN2", target_bir_lowering=False, num_devices=1)
    arrays, args = {}, []
    for name in _INS:
        a = _np.asarray(inputs[name])
        if name in _TRANSPOSED:
            a = a.T
        if a.ndim == 0:
            a = a.reshape(1)
        a = _np.ascontiguousarray(a)
        arrays[f"in_{name}_dram"] = a
        args.append(nc.dram_tensor(f"in_{name}_dram", a.shape, _mybir.dt.from_np(a.dtype), kind="ExternalInput").ap())
    res = nc.dram_tensor("out_0_dram", (L, NB, D), F32, kind="ExternalOutput").ap()
    decoder_layer(nc, *args, res)
    r = _run(nc, [arrays], core_ids=[0])
    return r.results[0]["out_0_dram"]
```

```python
from contextlib import ExitStack

import concourse.bass as bass
from concourse import mybir

F32 = mybir.dt.float32
F32R = mybir.dt.float32r
ALU = mybir.AluOpType
ACT = mybir.ActivationFunctionType
AX = mybir.AxisListType

P = 128
L = 32
NB = 256
D = 256
KT = D // P
NH = 16
DH = 64
HD = NH * DH
HC = HD // P
GB = P // L
SGT = 2
TOK = SGT * P
NSG = L * NB // TOK
NPROJ = 12
NQ = 77
LEAVES = 256
DEPTH = 8
EPS = 1e-5
SCORE_SCALE = DH ** -0.5
NX = SGT * GB
LO_ROW = 32


def above_zero(value):
    return not isinstance(value, int) or value > 0


def begun(b):
    return not isinstance(b, int) or b >= 0


def live(b):
    return not isinstance(b, int) or 0 <= b < L


def count(b):
    return min(b + 1, L) if isinstance(b, int) else b + 1


def f(ap):
    return ap.bitcast(F32)


def decoder_layer(nc, x, ctx_in, Wq, Wkv, Wo, w_cq, b_cq, w_c, b_c, w_q, b_q, WlT, b_l, fWq, routersT, leafT,
                  WoutT, Wout_b, out):
    with ExitStack() as top:
        def sem(name):
            return top.enter_context(nc.semaphore(name))

        yT = top.enter_context(nc.sbuf_tensor("yT", [P, KT, L * NB], F32))
        ident = top.enter_context(nc.sbuf_tensor("ident", [P, P], F32))
        neg_half = top.enter_context(nc.sbuf_tensor("neg_half", [P, 2], F32))
        s_ident0, s_ident = sem("ident_zeroed"), sem("ident_ready")
        attention(nc, sem, x, Wq, Wkv, Wo, yT, ident, neg_half, s_ident0, s_ident)
        cross_and_tree(nc, sem, ctx_in, w_cq, b_cq, w_c, b_c, w_q, b_q, WlT, b_l, fWq, routersT, leafT, WoutT,
                       Wout_b, yT, ident, neg_half, s_ident, out)


def attention(nc, sem, x, Wq, Wkv, Wo, yT, ident, neg_half, s_ident0, s_ident):
    with ExitStack() as ctx:
        def sb(name, shape, dt=F32):
            return ctx.enter_context(nc.sbuf_tensor(name, shape, dt))

        w_hi = sb("w_hi", [P, 3, KT, HD], F32R)
        w_lo = sb("w_lo", [P, 3, KT, HD], F32R)
        wo_hi = sb("wo_hi", [P, HC, D], F32R)
        wo_lo = sb("wo_lo", [P, HC, D], F32R)
        xT_hi = sb("xT_hi", [P, KT, TOK], F32R)
        xT_lo = sb("xT_lo", [P, KT, TOK], F32R)
        x_nat = [sb(f"x_nat{u}", [P, SGT, D]) for u in range(2)]
        qT = [sb(f"qT{u}", [P, HC, TOK]) for u in range(2)]
        kT = [sb(f"kT{u}", [P, HC, TOK]) for u in range(2)]
        v = [sb(f"v{u}", [P, SGT, HD]) for u in range(2)]
        prob = sb("prob", [P, NH, L])
        prob4 = prob[:].rearrange("p (r n) j -> p r n j", r=2)
        probT = sb("probT", [P, NH, P])
        rowmax = sb("rowmax", [P, NH])
        rowsum = sb("rowsum", [P, NH])
        rowinv = sb("rowinv", [P, NH])
        vecT_hi = sb("vecT_hi", [P, HC, P], F32R)
        vecT_lo = sb("vecT_lo", [P, HC, P], F32R)
        x_res = [sb(f"x_res{g}", [P, D]) for g in range(SGT)]
        res = sb("res", [P, D])
        y_nat = sb("y_nat", [P, D])
        stats = sb("stats", [P, 6])
        mv = sb("mv", [P, 2])
        veps = sb("veps", [P, 1])
        rstd = sb("rstd", [P, 1])

        wl, wsplit_hi, wsplit_lo, zeroed = sem("w_loaded"), sem("weights_hi_done"), sem("weights_lo_done"), sem("probT_zeroed")
        raw = [qT[0], kT[0], qT[1], kT[1]]
        with nc.Block() as block:
            @block.sync
            def _(sp):
                for j, src in enumerate((Wq, Wkv[:, 0:HD], Wkv[:, HD:2 * HD])):
                    sp.dma_start(raw[j][:].rearrange("p c t -> p (c t)").rearrange("p (k n) -> p k n", k=KT),
                                 src.rearrange("(k p) n -> p k n", p=P)).then_inc(wl, 16)
                sp.dma_start(raw[3][:], Wo.rearrange("(c p) n -> p c n", p=P)).then_inc(wl, 16)

            @block.scalar
            def _(act):
                act.wait_ge(wl, 64)
                for j in range(3):
                    act.activation(w_hi[:, j], raw[j][:].rearrange("p c t -> p (c t)").rearrange(
                        "p (k n) -> p k n", k=KT), ACT.Copy).then_inc(wsplit_hi, 1)
                act.activation(wo_hi[:], raw[3][:], ACT.Copy).then_inc(wsplit_hi, 1)

            @block.vector
            def _(dve):
                dve.memset(probT[:], 0.0).then_inc(zeroed, 1)
                dve.memset(neg_half[:], -0.5).then_inc(zeroed, 1)
                for j in range(3):
                    dve.wait_ge(wsplit_hi, j + 1)
                    dve.tensor_tensor(w_lo[:, j], raw[j][:].rearrange("p c t -> p (c t)").rearrange(
                        "p (k n) -> p k n", k=KT), f(w_hi[:, j]), ALU.subtract).then_inc(wsplit_lo, 1)
                dve.wait_ge(wsplit_hi, 4)
                dve.tensor_tensor(wo_lo[:], raw[3][:], f(wo_hi[:]), ALU.subtract).then_inc(wsplit_lo, 1)

            @block.gpsimd
            def _(pool):
                pool.memset(ident[:], 0.0).then_inc(s_ident0, 1)
                pool.wait_ge(s_ident0, 1)
                pool.affine_select(out=ident[:], in_=ident[:], compare_op=ALU.not_equal, fill=1.0, base=0,
                                   pattern=[[-1, P]], channel_multiplier=1).then_inc(s_ident, 1)

        def ps(name, shape):
            return ctx.enter_context(nc.psum_tensor(name, shape, F32))

        xT_ps = ps("xT_ps", [P, KT, TOK])
        proj_ps = [ps(f"proj_ps{u}", [P, 512]) for u in range(2)]
        score_ps = ps("score_ps", [P, 2, 512])
        s_view = score_ps[:, :, 0:NH // 2 * L].rearrange("p r (n j) -> p r n j", j=L)
        vecT_ps = ps("vecT_ps", [P, HC, P])
        oy_ps = ps("oy_ps", [P, 2, D])
        o_ps = oy_ps[:, 0, :]
        yT_ps = oy_ps[:, 1, :].rearrange("p (k t) -> p k t", k=KT)

        x_in = [sem(f"x_in{u}") for u in range(2)]
        res_in = [sem(f"res_in{g}") for g in range(SGT)]
        xT_done, xhi_done, xlo_done = sem("xT_done"), sem("xhi_done"), sem("xlo_done")
        proj_done, evac_act, evac_dve = sem("proj_done"), sem("evac_act"), sem("evac_dve")
        score_done, max_done, sub_done, exp_done = sem("score_done"), sem("max_done"), sem("sub_done"), sem("exp_done")
        sum_done, inv_done, prob_done, probT_done = sem("sum_done"), sem("inv_done"), sem("prob_done"), sem("probT_done")
        pv_done, vhi_done, vlo_done, o_done = sem("pv_done"), sem("vhi_done"), sem("vlo_done"), sem("o_done")
        res_done, st_done, mv_done, eps_done = sem("res_done"), sem("st_done"), sem("mv_done"), sem("eps_done")
        rstd_done, y_done, ytr_done, yT_done = sem("rstd_done"), sem("y_done"), sem("ytr_done"), sem("yT_done")

        def steps(eng, step):
            step(0, 0, 0, 2)
            step(1, 1, 0, 2)
            with eng.Fori(1, NSG // 2 - 1) as pair:
                step(pair * 2, 0, pair, 2)
                step(pair * 2 + 1, 1, pair, 2)
            step(NSG - 2, 0, NSG // 2 - 1, 1)
            step(NSG - 1, 1, NSG // 2 - 1, 0)

        with nc.Block() as block:
            @block.sync
            def _(sp):
                def load(s, u):
                    if above_zero(s - 1):
                        sp.wait_ge(xT_done, s - 1)
                    for g in range(SGT):
                        columns(x_nat[u][:, g, :], s, g, x_in[u])

                def columns(dst, s, g, landed):
                    for b in range(GB):
                        col = s * (SGT * GB) + (g * GB + b)
                        sp.dma_start(dst[b * L:(b + 1) * L, :], x[:, bass.ds(col, 1), :].rearrange(
                            "i a d -> i (a d)")).then_inc(landed, 16)

                def load_res(s):
                    for g in range(SGT):
                        if above_zero((s - 1) * SGT + g + 1):
                            sp.wait_ge(res_done, (s - 1) * SGT + g + 1)
                        columns(x_res[g], s, g, res_in[g])

                load(0, 0)
                load(1, 1)
                load_res(0)
                load(2, 0)
                load_res(1)
                load(3, 1)
                with sp.Fori(1, NSG // 2 - 1) as pair:
                    load_res(pair * 2)
                    load(pair * 2 + 2, 0)
                    load_res(pair * 2 + 1)
                    load(pair * 2 + 3, 1)
                load_res(NSG - 2)
                load_res(NSG - 1)

            @block.tensor
            def _(pe):
                def xtr(u, turn):
                    pe.wait_ge(x_in[u], turn * (16 * NX) + 16 * NX)
                    for k in range(KT):
                        for g in range(SGT):
                            ins = pe.transpose(xT_ps[:, k, g * P:(g + 1) * P], x_nat[u][:, g, k * P:(k + 1) * P],
                                               ident[:])
                    ins.then_inc(xT_done, 1)

                def proj(s, j):
                    if j == 0:
                        pe.wait_ge(xhi_done, s + 1)
                        pe.wait_ge(xlo_done, s + 1)
                    if above_zero(s * (NPROJ // 2) + j // 2):
                        pe.wait_ge(evac_dve if j % 2 else evac_act, s * (NPROJ // 2) + j // 2)
                    bank = proj_ps[j % 2]
                    if j < 8:
                        for h in range(2):
                            c = (2 * j + h) % HC
                            m = 0
                            for k in range(KT):
                                for w, t in ((w_hi, xT_hi), (w_hi, xT_lo), (w_lo, xT_hi)):
                                    ins = pe.matmul(bank[:, h * TOK:(h + 1) * TOK], w[:, j // 4, k, c * P:(c + 1) * P],
                                                    t[:, k, :], start=(m == 0), stop=(m == 5))
                                    m += 1
                    else:
                        g, h = (j - 8) // 2, (j - 8) % 2
                        m = 0
                        for k in range(KT):
                            for t, w in ((xT_hi, w_hi), (xT_hi, w_lo), (xT_lo, w_hi)):
                                ins = pe.matmul(bank[:], t[:, k, g * P:(g + 1) * P], w[:, 2, k, h * 512:(h + 1) * 512],
                                                start=(m == 0), stop=(m == 5))
                                m += 1
                    ins.then_inc(proj_done, 1)

                def scores(T, u, g):
                    if g:
                        pe.wait_ge(s_ident, 1)
                        if above_zero(T):
                            pe.wait_ge(sub_done, T)
                    for n in range(NH):
                        r = (n % 2) * DH
                        for b in range(GB):
                            t0 = g * P + b * L
                            ins = pe.matmul(s_view[b * L:(b + 1) * L, n % 2, n // 2, :], qT[u][r:r + DH, n // 2, t0:t0 + L],
                                            kT[u][r:r + DH, n // 2, t0:t0 + L], start=True, stop=True)
                    ins.then_inc(score_done, 1)

                def context(T, u, g):
                    pe.wait_ge(probT_done, T + 1)
                    if above_zero(T):
                        pe.wait_ge(vlo_done, T)
                    for n in range(NH):
                        r = (n % 2) * DH
                        ins = pe.matmul(vecT_ps[r:r + DH, n // 2, :], v[u][:, g, n * DH:(n + 1) * DH], probT[:, n % 2 * (NH // 2) + n // 2, :],
                                        start=True, stop=True)
                    ins.then_inc(pv_done, 1)

                def project_out(T):
                    pe.wait_ge(vlo_done, T + 1)
                    if above_zero(T):
                        pe.wait_ge(res_done, T)
                    if above_zero(T):
                        pe.wait_ge(yT_done, T)
                    m = 0
                    for c in range(HC):
                        for t, w in ((vecT_hi, wo_hi), (vecT_hi, wo_lo), (vecT_lo, wo_hi)):
                            ins = pe.matmul(o_ps, t[:, c, :], w[:, c, :], start=(m == 0), stop=(m == 3 * HC - 1))
                            m += 1
                    ins.then_inc(o_done, 1)

                def ytr(T):
                    pe.wait_ge(y_done, T + 1)
                    if above_zero(T):
                        pe.wait_ge(yT_done, T)
                    for k in range(KT):
                        ins = pe.transpose(yT_ps[:, k, :], y_nat[:, k * P:(k + 1) * P], ident[:])
                    ins.then_inc(ytr_done, 1)

                def step(s, u, pair, ahead):
                    nxt = s + 1
                    for g in range(SGT):
                        T = s * SGT + g
                        scores(T, u, g)
                        if ahead:
                            for j in range(6 * g, 6 * g + 4):
                                proj(nxt, j)
                        if above_zero(T):
                            project_out(T - 1)
                        if ahead:
                            for j in range(6 * g + 4, 6 * g + 6):
                                proj(nxt, j)
                        context(T, u, g)
                        if above_zero(T):
                            ytr(T - 1)
                    if ahead:
                        pe.wait_ge(evac_act, (s + 2) * (NPROJ // 2))
                        pe.wait_ge(evac_dve, (s + 2) * (NPROJ // 2))
                        pe.wait_ge(sub_done, s * SGT + SGT)
                    if ahead == 2:
                        xtr(u, pair + 1)

                pe.wait_ge(s_ident, 1)
                xtr(0, 0)
                for j in range(NPROJ):
                    proj(0, j)
                pe.wait_ge(evac_act, NPROJ // 2)
                pe.wait_ge(evac_dve, NPROJ // 2)
                xtr(1, 0)
                steps(pe, step)
                project_out(2 * NSG - 1)
                ytr(2 * NSG - 1)

            def evacuated_to(s_parity, j):
                if j < 8:
                    dst = (qT, kT)[j // 4][s_parity]
                    return dst[:, 2 * (j % 4):2 * (j % 4) + 2, :].rearrange("p c t -> p (c t)")
                g, h = (j - 8) // 2, (j - 8) % 2
                return v[s_parity][:, g, h * 512:(h + 1) * 512]

            @block.scalar
            def _(act):
                def xhi(s):
                    act.wait_ge(xT_done, s + 1)
                    if above_zero(s * NPROJ):
                        act.wait_ge(proj_done, s * NPROJ)
                    act.activation(xT_hi[:], xT_ps[:], ACT.Copy).then_inc(xhi_done, 1)

                def evac(s, u, j):
                    act.wait_ge(proj_done, s * NPROJ + (j + 1))
                    act.activation(evacuated_to(u, j), proj_ps[0][:], ACT.Copy).then_inc(evac_act, 1)

                def yT_copy(T):
                    act.wait_ge(ytr_done, T + 1)
                    dst = yT[:].rearrange("p k (i b) -> p k i b", i=L)
                    for k in range(KT):
                        act.activation(dst[:, k, :, bass.ds(T * GB, GB)],
                                       yT_ps[:, k, :].rearrange("p (b i) -> p i b", b=GB),
                                       ACT.Copy).then_inc(yT_done, 1) if k == KT - 1 else \
                            act.activation(dst[:, k, :, bass.ds(T * GB, GB)],
                                           yT_ps[:, k, :].rearrange("p (b i) -> p i b", b=GB), ACT.Copy)

                def step(s, u, pair, ahead):
                    for g in range(SGT):
                        T = s * SGT + g
                        act.wait_ge(sub_done, T + 1)
                        act.activation(prob[:], prob[:], ACT.Exp, scale=SCORE_SCALE).then_inc(exp_done, 1)
                        if ahead:
                            evac(s + 1, 1 - u, 6 * g)
                            evac(s + 1, 1 - u, 6 * g + 2)
                            evac(s + 1, 1 - u, 6 * g + 4)
                        act.wait_ge(pv_done, T + 1)
                        if above_zero(T):
                            act.wait_ge(o_done, T)
                        act.activation(vecT_hi[:], vecT_ps[:], ACT.Copy).then_inc(vhi_done, 1)
                        if above_zero(T):
                            yT_copy(T - 1)
                    if ahead == 2:
                        xhi(s + 2)

                xhi(0)
                for j in range(0, NPROJ, 2):
                    evac(0, 0, j)
                xhi(1)
                steps(act, step)
                yT_copy(2 * NSG - 1)

            @block.vector
            def _(dve):
                def xlo(s):
                    dve.wait_ge(xhi_done, s + 1)
                    dve.tensor_tensor(xT_lo[:], xT_ps[:], f(xT_hi[:]), ALU.subtract).then_inc(xlo_done, 1)

                def evac(s, u, j):
                    dve.wait_ge(proj_done, s * NPROJ + (j + 1))
                    dve.tensor_copy(evacuated_to(u, j), proj_ps[1][:]).then_inc(evac_dve, 1)

                def norm(s, T, g):
                    dve.wait_ge(res_in[g], (s + 1) * (16 * GB))
                    dve.wait_ge(o_done, T + 1)
                    dve.tensor_tensor(res[:], o_ps, x_res[g][:], ALU.add).then_inc(res_done, 1)
                    dve.wait_ge(res_done, T + 1)
                    dve.bn_stats(stats[:], res[:]).then_inc(st_done, 1)
                    dve.wait_ge(s_ident, 1)
                    dve.wait_ge(st_done, T + 1)
                    dve.bn_aggr(mv[:], stats[:]).then_inc(mv_done, 1)
                    dve.wait_ge(mv_done, T + 1)
                    dve.tensor_scalar(veps[:], mv[:, 1:2], EPS, None, ALU.add).then_inc(eps_done, 1)

                def norm_out(T):
                    dve.wait_ge(rstd_done, T + 1)
                    if above_zero(T):
                        dve.wait_ge(ytr_done, T)
                    dve.tensor_scalar(y_nat[:], res[:], mv[:, 0:1], rstd[:], ALU.subtract, ALU.mult).then_inc(y_done, 1)

                def step(s, u, pair, ahead):
                    for g in range(SGT):
                        T = s * SGT + g
                        dve.wait_ge(score_done, T + 1)
                        dve.tensor_reduce(rowmax[:].rearrange("p (r n) -> p r n", r=2), s_view, AX.X, ALU.max).then_inc(max_done, 1)
                        dve.wait_ge(max_done, T + 1)
                        dve.tensor_tensor(prob4, s_view, rowmax[:].rearrange("p (r n) -> p r n", r=2).unsqueeze(3)
                                          .broadcast_to([P, 2, NH // 2, L]), ALU.subtract).then_inc(sub_done, 1)
                        if ahead:
                            evac(s + 1, 1 - u, 6 * g + 1)
                        dve.wait_ge(exp_done, T + 1)
                        dve.tensor_reduce(rowsum[:], prob[:], AX.X, ALU.add).then_inc(sum_done, 1)
                        dve.wait_ge(sum_done, T + 1)
                        dve.reciprocal(rowinv[:], rowsum[:]).then_inc(inv_done, 1)
                        if ahead:
                            evac(s + 1, 1 - u, 6 * g + 3)
                        dve.wait_ge(prob_done, T + 1)
                        if above_zero(T):
                            dve.wait_ge(pv_done, T)
                        for b in range(GB):
                            ins = dve.transpose(probT[b * L:(b + 1) * L, :, b * L:(b + 1) * L],
                                                prob[b * L:(b + 1) * L, :, :])
                        ins.then_inc(probT_done, 1)
                        if above_zero(T):
                            norm(s - (1 - g), T - 1, 1 - g)
                            norm_out(T - 1)
                        if ahead:
                            evac(s + 1, 1 - u, 6 * g + 5)
                        dve.wait_ge(vhi_done, T + 1)
                        dve.tensor_tensor(vecT_lo[:], vecT_ps[:], f(vecT_hi[:]), ALU.subtract).then_inc(vlo_done, 1)
                    if ahead == 2:
                        xlo(s + 2)

                xlo(0)
                for j in range(1, NPROJ, 2):
                    evac(0, 0, j)
                xlo(1)
                steps(dve, step)
                norm(NSG - 1, 2 * NSG - 1, 1)
                norm_out(2 * NSG - 1)

            @block.gpsimd
            def _(pool):
                def rstd_of(T):
                    pool.wait_ge(eps_done, T + 1)
                    pool.tensor_tensor(rstd[:], veps[:], neg_half[:, 0:1], ALU.pow).then_inc(rstd_done, 1)

                def step(s, u, pair, ahead):
                    for g in range(SGT):
                        T = s * SGT + g
                        pool.wait_ge(inv_done, T + 1)
                        pool.tensor_tensor(prob[:], prob[:], rowinv[:].unsqueeze(2).broadcast_to([P, NH, L]),
                                           ALU.mult).then_inc(prob_done, 1)
                        if above_zero(T):
                            rstd_of(T - 1)

                steps(pool, step)
                rstd_of(2 * NSG - 1)


def cross_and_tree(nc, sem, ctx_in, w_cq, b_cq, w_c, b_c, w_q, b_q, WlT, b_l, fWq, routersT, leafT, WoutT, Wout_b,
                   yT, ident, neg_half, s_ident, out):
    NGATE = routersT.shape[1]
    CT = NB // P
    with ExitStack() as ctx:
        def sb(name, shape, dt=F32):
            return ctx.enter_context(nc.sbuf_tensor(name, shape, dt))

        def ps(name, shape):
            return ctx.enter_context(nc.psum_tensor(name, shape, F32))

        def halves(name, shape, n):
            return [(sb(f"{name}_hi{u}", shape, F32R), sb(f"{name}_lo{u}", shape, F32R)) for u in range(n)]

        wl_raw = sb("wl_raw", [P, 4, KT, D])
        w1_id = sb("w1_id", [P, KT, D])
        [(w2_hi, w2_lo)] = halves("w2", [P, KT, D], 1)
        [(w3_hi, w3_lo)] = halves("w3", [P, KT, D], 1)
        fwq = sb("fwq", [P, KT, D])
        routers = sb("routers", [P, KT, LEAVES])
        leaf_v = sb("leaf_v", [P, KT, LEAVES])
        wout = sb("wout", [P, KT, D])
        gate_w = sb("gate_w", [P, KT, LEAVES])
        leaf_w = sb("leaf_w", [P, KT, D])
        [(gate_hi, gate_lo)] = halves("gate", [P, KT, LEAVES], 1)
        [(leafw_hi, leafw_lo)] = halves("leafw", [P, KT, D], 1)
        vec3 = sb("vec3", [P, 3, KT])
        consts = sb("consts", [P, 3])
        const = sb("const", [P, 1])
        wq_rows = sb("wq_rows", [P, KT, P])
        ones = sb("ones", [P, P])
        ones_r = sb("ones_r", [P, P], F32R)
        bias_raw = sb("bias_raw", [P, 2, D])
        bias_r = sb("bias_r", [P, 2, D], F32R)

        q_nat = [sb(f"q_nat{u}", [NQ, D]) for u in range(2)]
        qT = sb("cqT", [P, KT, NQ])
        g_mat = sb("g_mat", [P, KT, NQ])
        c = [sb(f"c{u}", [P, KT, NB]) for u in range(2)]
        c_r = halves("c", [P, KT, NB], 2)
        u_r = halves("u", [P, KT, NB], 2)
        w_r = halves("w", [P, KT, NB], 2)
        we_r = halves("we", [P, KT, D], 2)
        w32 = sb("w32", [P, KT, NB])
        we32 = sb("we32", [P, KT, D])
        a_sb = sb("a_sb", [P, CT, NQ])
        aT = sb("aT", [NQ, NB])
        neg_smax = sb("neg_smax", [P, CT])
        smax = sb("smax", [P, CT])
        ssum = sb("ssum", [P, CT])
        sinv = sb("sinv", [P, CT])
        diag = sb("diag", [P, CT, P])
        neg_m = sb("neg_m", [P, 1])
        eb = sb("eb", [P, NB])
        ebsum = sb("ebsum", [P, 1])
        ebinv = sb("ebinv", [P, 1])
        scratch = sb("scratch", [P, KT, NB])
        q2_raw = sb("q2_raw", [P, KT])
        q2 = sb("q2", [P, KT])
        y2 = [sb(f"y2_{u}", [P, CT, D]) for u in range(2)]
        [(y2T_hi, y2T_lo)] = halves("y2T", [P, KT, NB], 1)
        th = sb("th", [P, CT, LEAVES])
        lv = [sb(f"lv{u}", [P, CT, LEAVES // 2]) for u in range(2)]
        leaf = sb("leaf", [P, CT, LEAVES])
        [(lT_hi, lT_lo)] = halves("lT", [P, KT, NB], 1)
        r3 = sb("r3", [P, CT, D])
        y3 = [sb(f"y3_{u}", [P, CT, D]) for u in range(2)]
        st = [sb(f"st{n}", [P, CT, 6]) for n in (2, 3)]
        mv = [sb(f"mv{n}", [P, CT, 2]) for n in (2, 3)]
        veps = [sb(f"veps{n}", [P, CT]) for n in (2, 3)]
        rstd = [sb(f"rstd{n}", [P, CT]) for n in (2, 3)]
        shift = [sb(f"shift{n}", [P, CT]) for n in (2, 3)]

        s_bank = ps("s_ps", [P, 512])
        out_ps = ps("out_ps", [P, CT, D])
        turned_ps = ps("turned_ps", [P, KT, NB])
        z_bank = [ps(f"z_ps{ct}", [P, 512]) for ct in range(CT)]
        z_ps = [bank[:, 0:D] for bank in z_bank]
        aq_ps = ps("aq_ps", [P, 512])
        c2q_ps = ps("c2q_ps", [P, KT, NB])
        gate_bc_ps = ps("gate_bc_ps", [P, 512])
        gate_ps = gate_bc_ps[:].rearrange("p (c n) -> p c n", c=CT)
        bc_ps = gate_bc_ps[:, 0:NB]
        s_ps = s_bank[:, 0:CT * NQ].rearrange("p (c q) -> p c q", c=CT)
        aT_ps = aq_ps[:, 0:NB]
        qT_ps = aq_ps[:, NB:NB + KT * NQ].rearrange("p (k q) -> p k q", k=KT)

        ld, fused, setup = sem("c_loaded"), sem("c_fused"), sem("c_setup")
        setup_v = [0]
        NLOADS = 15
        with nc.allow_non_contiguous_dma("small vectors"), nc.Block() as block:
            @block.sync
            def _(sp):
                sp.dma_start(wl_raw[:], WlT.rearrange("(f k p) e -> p f k e", f=4, p=P)).then_inc(ld, 16)
                sp.dma_start(fwq[:], fWq.rearrange("(k p) d -> p k d", p=P)).then_inc(ld, 16)
                sp.dma_start(routers[:, :, 0:NGATE], routersT.rearrange("(k p) m -> p k m", p=P)).then_inc(ld, 16)
                sp.dma_start(leaf_v[:], leafT.rearrange("(k p) m -> p k m", p=P)).then_inc(ld, 16)
                sp.dma_start(wout[:], WoutT.rearrange("(k p) e -> p k e", p=P)).then_inc(ld, 16)
                for n, w in enumerate((w_cq, w_c, w_q)):
                    sp.dma_start(vec3[:, n, :], w.rearrange("(k p) -> p k", p=P)).then_inc(ld, 16)
                for n, b in enumerate((b_cq, b_c, b_q)):
                    sp.dma_start(consts[:, n:n + 1], b.partition_broadcast(P)).then_inc(ld, 16)
                sp.wait_ge(setup, 1)
                for row in (0, LO_ROW):
                    for n, b in enumerate((b_l, Wout_b)):
                        sp.dma_start(bias_raw[row:row + 1, n, :], b.rearrange("(a e) -> a e", a=1)).then_inc(ld, 16)

            @block.tensor
            def _(pe):
                pe.wait_ge(ld, 16 * NLOADS)
                pe.wait_ge(setup, 2)
                for k in range(KT):
                    for e in range(KT):
                        pe.matmul(z_ps[k], fwq[:, e, k * P:(k + 1) * P], routers[:, e, :], start=(e == 0),
                                  stop=(e == KT - 1))
                for k in range(KT):
                    for e in range(KT):
                        ins = pe.matmul(c2q_ps[:, k, :], leaf_v[:, e, k * P:(k + 1) * P], wout[:, e, :],
                                        start=(e == 0), stop=(e == KT - 1))
                ins.then_inc(fused, 1)

            @block.vector
            def _(dve):
                def chain(ins):
                    setup_v[0] += 1
                    ins.then_inc(setup, 1)
                    dve.wait_ge(setup, setup_v[0])

                chain(dve.memset(bias_raw[:], 0.0))
                chain(dve.memset(routers[:, :, NGATE:LEAVES], 0.0))
                dve.wait_ge(ld, 16 * NLOADS)
                chain(dve.memset(ones[:], 1.0))
                chain(dve.tensor_copy(ones_r[:], ones[:]))
                for k in range(KT):
                    chain(dve.tensor_scalar(wq_rows[:, k, :], ones[:], vec3[:, 2, k:k + 1], None, ALU.mult))
                chain(dve.tensor_tensor(const[:], consts[:, 0:1], consts[:, 1:2], ALU.add))
                chain(dve.tensor_tensor(const[:], const[:], consts[:, 2:3], ALU.add))
                chain(dve.tensor_copy(w1_id[:], wl_raw[:, 0]))
                for k in range(KT):
                    part = w1_id[:, k, k * P:(k + 1) * P]
                    chain(dve.tensor_tensor(part, part, ident[:], ALU.add))
                chain(dve.tensor_copy(bias_r[:], bias_raw[:]))
                low = slice(LO_ROW, LO_ROW + 1)
                chain(dve.tensor_tensor(bias_r[low], bias_raw[low], f(bias_r[low]), ALU.subtract))
                for src, hi, lo in ((wl_raw[:, 1], w2_hi, w2_lo), (wl_raw[:, 2], w3_hi, w3_lo)):
                    chain(dve.tensor_copy(hi[:], src))
                    chain(dve.tensor_tensor(lo[:], src, f(hi[:]), ALU.subtract))
                dve.wait_ge(fused, 1)
                for k in range(KT):
                    chain(dve.tensor_copy(gate_w[:, k, :], z_ps[k]))
                chain(dve.tensor_scalar(leaf_w[:], c2q_ps[:], 2.0 ** -DEPTH, None, ALU.mult))
                for src, hi, lo in ((gate_w, gate_hi, gate_lo), (leaf_w, leafw_hi, leafw_lo)):
                    chain(dve.tensor_copy(hi[:], src[:]))
                    chain(dve.tensor_tensor(lo[:], src[:], f(hi[:]), ALU.subtract))

        q_in = [sem(f"q_in{u}") for u in range(2)]
        c_in = [sem(f"c_in{u}") for u in range(2)]
        gate_done = sem("gate_done")
        scores_done = sem("scores_done")
        z_done = [sem(f"z_done{ct}") for ct in range(CT)]
        maxrow_done = sem("maxrow_done")
        aTr_done = sem("aTr_done")
        leafTr_done = sem("leafTr_done")
        c2q_done = sem("c2q_done")
        y2Tr_done = sem("y2Tr_done")
        qTr_done = sem("qTr_done")
        tree_done = sem("tree_done")
        tanh_done = sem("tanh_done")
        a_exp_done = sem("a_exp_done")
        b_exp_done = sem("b_exp_done")
        aT_copied = sem("aT_copied")
        lT_hi_done = sem("lT_hi_done")
        we_hi_done = sem("we_hi_done")
        u_hi_done = sem("u_hi_done")
        w_hi_done = sem("w_hi_done")
        y2T_hi_done = sem("y2T_hi_done")
        g_mat_done = sem("g_mat_done")
        c_hi_done = sem("c_hi_done")
        neg_smax_done = sem("neg_smax_done")
        smax_done = sem("smax_done")
        diag_done = sem("diag_done")
        sinv_done = sem("sinv_done")
        a_done = sem("a_done")
        z_stats_done = sem("z_stats_done")
        z_mean_done = sem("z_mean_done")
        z_var_done = sem("z_var_done")
        z_shift_done = sem("z_shift_done")
        y2_done = sem("y2_done")
        neg_m_done = sem("neg_m_done")
        q2_sum_done = sem("q2_sum_done")
        eb_inv_done = sem("eb_inv_done")
        q2_done = sem("q2_done")
        we_done = sem("we_done")
        u_lo_done = sem("u_lo_done")
        w_done = sem("w_done")
        lT_lo_done = sem("lT_lo_done")
        y2T_lo_done = sem("y2T_lo_done")
        qT_copied = sem("qT_copied")
        c_lo_done = sem("c_lo_done")
        res3_done = sem("res3_done")
        r3_stats_done = sem("r3_stats_done")
        r3_mean_done = sem("r3_mean_done")
        r3_var_done = sem("r3_var_done")
        r3_shift_done = sem("r3_shift_done")
        y3_done = sem("y3_done")
        leaves_done = sem("leaves_done")
        rstd2_done = sem("rstd2_done")
        we_lo_done = sem("we_lo_done")
        w_lo_done = sem("w_lo_done")
        rstd3_done = sem("rstd3_done")
        level_done = sem("level_done")
        y_out = [sem(f"y_out{u}") for u in range(2)]
        NLV = DEPTH - 1

        def steps(eng, step):
            for t in range(-2, 4):
                step(t, t % 2, t // 2)
            with eng.Fori(2, L // 2 - 1) as pair:
                step(pair * 2, 0, pair)
                step(pair * 2 + 1, 1, pair)
            for t in range(L - 2, L + 2):
                step(t, t % 2, t // 2)

        with nc.Block() as block:
            @block.sync
            def _(sp):
                def load(b, u):
                    if begun(b - 2):
                        sp.wait_ge(c2q_done, count(b - 2))
                    sp.dma_start(q_nat[u][:], ctx_in[bass.ds(b, 1), :, :].rearrange("a q d -> (a q) d"))\
                        .then_inc(q_in[u], 16)

                def load_c(b, u):
                    if begun(b - 2):
                        sp.wait_ge(scores_done, count(b - 2))
                    if begun(b - 2):
                        sp.wait_ge(c_lo_done, count(b - 2))
                    if begun(b - 2):
                        sp.wait_ge(q2_sum_done, count(b - 2))
                    if begun(b - 2):
                        sp.wait_ge(w_done, count(b - 2))
                    sp.dma_start(c[u][:], yT[:, :, bass.ds(b * NB, NB)]).then_inc(c_in[u], 16)

                def store(b, u):
                    sp.wait_ge(y3_done, count(b))
                    for ct in range(CT):
                        sp.dma_start(out[bass.ds(b, 1), ct * P:(ct + 1) * P, :].rearrange("a c d -> (a c) d"),
                                     y3[u][:, ct, :]).then_inc(y_out[u], 16)

                def step(t, u, pair):
                    if live(t + 2):
                        load_c(t + 2, u)
                    if live(t - 2):
                        store(t - 2, u)
                    if live(t + 3):
                        load(t + 3, 1 - u)

                load(0, 0)
                for t in range(-2, 4):
                    step(t, t % 2, t // 2)
                with sp.Fori(2, L // 2 - 2) as pair:
                    step(pair * 2, 0, pair)
                    step(pair * 2 + 1, 1, pair)
                for t in range(L - 4, L + 2):
                    step(t, t % 2, t // 2)
                for u in range(2):
                    sp.wait_ge(y_out[u], 16 * CT * (L // 2))

            @block.tensor
            def _(pe):
                def three(dst, lt, rt, first, last):
                    m = 0
                    for k in range(KT):
                        for a, b in ((0, 0), (0, 1), (1, 0)):
                            ins = pe.matmul(dst, lt(a, k), rt(b, k), start=(first and m == 0),
                                            stop=(last and m == 3 * KT - 1))
                            m += 1
                    return ins

                def add_bias(dst, n):
                    return pe.matmul(dst, ones_r[:], bias_r[:, n, :], start=False, stop=True)

                def step(t, u, pair):
                    v_ = 1 - u
                    if live(t + 1):
                        pe.wait_ge(c_in[v_], (pair + u) * 16 + 16)
                        pe.wait_ge(g_mat_done, count(t + 1))
                        if begun(t):
                            pe.wait_ge(a_exp_done, count(t))
                        for k in range(KT):
                            pe.matmul(s_ps, wq_rows[:, k, :], qT[:, k, :].unsqueeze(1).broadcast_to([P, CT, NQ]),
                                      start=(k == 0), stop=False)
                        for ct in range(CT):
                            for k in range(KT):
                                ins = pe.matmul(s_ps[:, ct, :], c[v_][:, k, ct * P:(ct + 1) * P], g_mat[:, k, :],
                                                start=False, stop=(ct == CT - 1 and k == KT - 1))
                        ins.then_inc(scores_done, 1)
                    if live(t - 1):
                        pe.wait_ge(y2T_hi_done, count(t - 1))
                        pe.wait_ge(y2T_lo_done, count(t - 1))
                        if live(t):
                            pe.wait_ge(b_exp_done, count(t))
                        for ct in range(CT):
                            ins = three(gate_ps[:, ct, :], lambda a, k: (y2T_hi, y2T_lo)[a][:, k, ct * P:(ct + 1) * P],
                                        lambda b, k: (gate_hi, gate_lo)[b][:, k, :], True, True)
                        ins.then_inc(gate_done, 1)

                    def project(ct):
                        sl = slice(ct * P, (ct + 1) * P)
                        if ct == 0:
                            pe.wait_ge(u_hi_done, count(t))
                            pe.wait_ge(u_lo_done, count(t))
                            if begun(t - 1):
                                pe.wait_ge(y2_done, count(t - 1))
                        three(z_ps[ct], lambda a, k: u_r[u][a][:, k, sl],
                              lambda b, k: (w2_hi, w2_lo)[b][:, k, :], True, False)
                        if ct == 0:
                            pe.wait_ge(c_lo_done, count(t))
                            pe.wait_ge(we_lo_done, count(t))
                        three(z_ps[ct], lambda a, k: c_r[u][a][:, k, sl], lambda b, k: we_r[u][b][:, k, :],
                              False, False)
                        if ct == 0:
                            pe.wait_ge(w_lo_done, count(t))
                        three(z_ps[ct], lambda a, k: w_r[u][a][:, k, sl],
                              lambda b, k: (w3_hi, w3_lo)[b][:, k, :], False, False)
                        return add_bias(z_ps[ct], 0)

                    if live(t):
                        project(0).then_inc(z_done[0], 1)
                    if live(t + 1):
                        pe.wait_ge(a_done, count(t + 1))
                        pe.wait_ge(g_mat_done, count(t + 1))
                        if begun(t):
                            pe.wait_ge(aT_copied, count(t))
                        for ct in range(CT):
                            ins = pe.transpose(aT_ps[0:NQ, ct * P:(ct + 1) * P], a_sb[:, ct, :], ident[:])
                        ins.then_inc(aTr_done, 1)
                        pe.wait_ge(diag_done, count(t + 1))
                        if begun(t):
                            pe.wait_ge(b_exp_done, count(t))
                        if live(t - 1):
                            pe.wait_ge(tanh_done, count(t - 1))
                        pe.matmul(bc_ps, ones[:], diag[:].rearrange("p c t -> p (c t)"), start=True,
                                  stop=True).then_inc(maxrow_done, 1)
                    if live(t):
                        project(1).then_inc(z_done[1], 1)
                    if live(t - 1):
                        pe.wait_ge(leaves_done, count(t - 1))
                        pe.wait_ge(y2T_lo_done, count(t - 1))
                        for k in range(KT):
                            for ct in range(CT):
                                ins = pe.transpose(turned_ps[:, k, ct * P:(ct + 1) * P], leaf[:, ct, k * P:(k + 1) * P],
                                                   ident[:])
                        ins.then_inc(leafTr_done, 1)
                    if live(t + 1):
                        pe.wait_ge(aT_copied, count(t + 1))
                        if begun(t):
                            pe.wait_ge(u_lo_done, count(t))
                        if begun(t):
                            pe.wait_ge(w_done, count(t))
                        for k in range(KT):
                            ins = pe.matmul(c2q_ps[:, k, :], q_nat[v_][:, k * P:(k + 1) * P], aT[:], start=True, stop=True)
                        ins.then_inc(c2q_done, 1)
                    if live(t + 2):
                        pe.wait_ge(q_in[u], pair * 16 + 32)
                        if begun(t + 1):
                            pe.wait_ge(g_mat_done, count(t + 1))
                        if begun(t + 1):
                            pe.wait_ge(aT_copied, count(t + 1))
                        for k in range(KT):
                            ins = pe.transpose(qT_ps[:, k, :], q_nat[u][:, k * P:(k + 1) * P], ident[0:NQ, 0:NQ])
                        ins.then_inc(qTr_done, 1)
                    if live(t - 1):
                        pe.wait_ge(lT_hi_done, count(t - 1))
                        pe.wait_ge(lT_lo_done, count(t - 1))
                        if begun(t - 2):
                            pe.wait_ge(res3_done, count(t - 2))
                        for ct in range(CT):
                            three(out_ps[:, ct, :], lambda a, k: (lT_hi, lT_lo)[a][:, k, ct * P:(ct + 1) * P],
                                  lambda b, k: (leafw_hi, leafw_lo)[b][:, k, :], True, False)
                            ins = add_bias(out_ps[:, ct, :], 1)
                        ins.then_inc(tree_done, 1)
                    if live(t):
                        pe.wait_ge(y2_done, count(t))
                        if begun(t - 1):
                            pe.wait_ge(lT_lo_done, count(t - 1))
                        for k in range(KT):
                            for ct in range(CT):
                                ins = pe.transpose(turned_ps[:, k, ct * P:(ct + 1) * P], y2[u][:, ct, k * P:(k + 1) * P],
                                                   ident[:])
                        ins.then_inc(y2Tr_done, 1)

                steps(pe, step)

            @block.scalar
            def _(act):
                def step(t, u, pair):
                    v_ = 1 - u
                    if live(t + 1):
                        act.wait_ge(c_in[v_], (pair + u) * 16 + 16)
                        if begun(t - 1):
                            act.wait_ge(z_done[1], count(t - 1))
                        act.activation(c_r[v_][0][:], c[v_][:], ACT.Copy).then_inc(c_hi_done, 1)
                        act.wait_ge(neg_smax_done, count(t + 1))
                        if begun(t):
                            act.wait_ge(aTr_done, count(t))
                        for ct in range(CT):
                            ins = act.activation(a_sb[:, ct, :], s_ps[:, ct, :], ACT.Exp, bias=neg_smax[:, ct:ct + 1],
                                                 accum_out=ssum[:, ct:ct + 1])
                        ins.then_inc(a_exp_done, 1)
                    if live(t - 1):
                        act.wait_ge(gate_done, count(t - 1))
                        if begun(t - 2):
                            act.wait_ge(leaves_done, count(t - 2))
                        act.activation(th[:], gate_ps, ACT.Tanh, scale=0.5).then_inc(tanh_done, 1)
                    if live(t + 1):
                        act.wait_ge(smax_done, count(t + 1))
                        if begun(t):
                            act.wait_ge(maxrow_done, count(t))
                        for ct in range(CT):
                            ins = act.activation(diag[:, ct, :], ident[:], ACT.Copy, scale=smax[:, ct:ct + 1])
                        ins.then_inc(diag_done, 1)
                    if live(t - 2):
                        act.wait_ge(r3_shift_done, count(t - 2))
                        if above_zero(pair - 1 - 1):
                            act.wait_ge(y_out[u], pair * (16 * CT) - 16 * CT)
                        for ct in range(CT):
                            ins = act.activation(y3[u][:, ct, :], r3[:, ct, :], ACT.Identity,
                                                 scale=rstd[1][:, ct:ct + 1], bias=shift[1][:, ct:ct + 1])
                        ins.then_inc(y3_done, 1)
                    if live(t + 1):
                        act.wait_ge(aTr_done, count(t + 1))
                        if begun(t):
                            act.wait_ge(c2q_done, count(t))
                        act.activation(aT[:], aT_ps[0:NQ, :], ACT.Copy).then_inc(aT_copied, 1)
                        act.wait_ge(neg_m_done, count(t + 1))
                        if begun(t):
                            act.wait_ge(q2_done, count(t))
                        act.activation(eb[:], bc_ps, ACT.Exp, bias=neg_m[:], accum_out=ebsum[:])\
                            .then_inc(b_exp_done, 1)
                    if live(t - 1):
                        act.wait_ge(leafTr_done, count(t - 1))
                        if begun(t - 2):
                            act.wait_ge(tree_done, count(t - 2))
                        act.activation(lT_hi[:], turned_ps[:], ACT.Copy).then_inc(lT_hi_done, 1)
                    if live(t + 1):
                        act.wait_ge(c2q_done, count(t + 1))
                        act.activation(u_r[v_][0][:], c2q_ps[:], ACT.Copy).then_inc(u_hi_done, 1)
                    if live(t + 2):
                        act.wait_ge(qTr_done, count(t + 2))
                        if begun(t + 1):
                            act.wait_ge(scores_done, count(t + 1))
                        act.activation(qT[:], qT_ps, ACT.Copy)
                        for k in range(KT):
                            ins = act.activation(g_mat[:, k, :], qT_ps[:, k, :], ACT.Identity, scale=vec3[:, 0, k:k + 1],
                                                 bias=vec3[:, 1, k:k + 1])
                        ins.then_inc(g_mat_done, 1)
                    if live(t):
                        act.wait_ge(z_shift_done, count(t))
                        if begun(t - 2):
                            act.wait_ge(y2Tr_done, count(t - 2))
                        if begun(t - 2):
                            act.wait_ge(res3_done, count(t - 2))
                        for ct in range(CT):
                            ins = act.activation(y2[u][:, ct, :], z_ps[ct], ACT.Identity,
                                                 scale=rstd[0][:, ct:ct + 1], bias=shift[0][:, ct:ct + 1])
                        ins.then_inc(y2_done, 1)
                    if live(t + 1):
                        act.wait_ge(we_done, count(t + 1))
                        act.activation(we_r[v_][0][:], we32[:], ACT.Copy).then_inc(we_hi_done, 1)
                    if live(t):
                        act.wait_ge(y2Tr_done, count(t))
                        if begun(t - 1):
                            act.wait_ge(gate_done, count(t - 1))
                        act.activation(y2T_hi[:], turned_ps[:], ACT.Copy).then_inc(y2T_hi_done, 1)
                    if live(t + 1):
                        act.wait_ge(w_done, count(t + 1))
                        act.activation(w_r[v_][0][:], w32[:], ACT.Copy).then_inc(w_hi_done, 1)

                steps(act, step)

            @block.vector
            def _(dve):
                def mean_var(n, b, stats_done, mean_done, var_done):
                    dve.wait_ge(s_ident, 1)
                    dve.wait_ge(stats_done, count(b))
                    for ct in range(CT):
                        ins = dve.bn_aggr(mv[n][:, ct, :], st[n][:, ct, :])
                    ins.then_inc(mean_done, 1)
                    dve.wait_ge(mean_done, count(b))
                    dve.tensor_scalar(veps[n][:], mv[n][:, :, 1], EPS, None, ALU.add).then_inc(var_done, 1)

                def leaves(b, between):
                    dve.wait_ge(tanh_done, count(b))
                    dve.tensor_scalar(lv[0][:, :, 0:1], th[:, :, 0:1], -1.0, 1.0, ALU.mult, ALU.add)
                    dve.tensor_scalar(lv[0][:, :, 1:2], th[:, :, 0:1], 1.0, None, ALU.add).then_inc(level_done, 1)
                    src = lv[0]
                    for level in range(1, DEPTH):
                        n = 2 ** level
                        last = level == DEPTH - 1
                        if level in between:
                            between[level]()
                        if last:
                            if begun(b - 1):
                                dve.wait_ge(leafTr_done, count(b - 1))
                        dst = leaf if last else lv[level % 2]
                        kids = dst[:, :, 0:2 * n].rearrange("p c (m two) -> p c m two", two=2)
                        dve.wait_ge(level_done, b * NLV + level)
                        dve.scalar_tensor_tensor(kids[:, :, :, 0], th[:, :, n - 1:2 * n - 1], 1.0, src[:, :, 0:n],
                                                 ALU.subtract, ALU.mult, reverse0=True)
                        dve.scalar_tensor_tensor(kids[:, :, :, 1], th[:, :, n - 1:2 * n - 1], 1.0, src[:, :, 0:n],
                                                 ALU.add, ALU.mult).then_inc(leaves_done if last else level_done, 1)
                        src = dst

                def step(t, u, pair):
                    v_ = 1 - u
                    if live(t + 1):
                        dve.wait_ge(scores_done, count(t + 1))
                        if begun(t):
                            dve.wait_ge(a_exp_done, count(t))
                        dve.tensor_reduce(neg_smax[:], s_ps, AX.X, ALU.max, negate=True).then_inc(neg_smax_done, 1)
                    if live(t - 2):
                        dve.wait_ge(res3_done, count(t - 2))
                        for ct in range(CT):
                            ins = dve.bn_stats(st[1][:, ct, :], r3[:, ct, :])
                        ins.then_inc(r3_stats_done, 1)
                    if live(t + 1):
                        dve.wait_ge(neg_smax_done, count(t + 1))
                        if begun(t):
                            dve.wait_ge(diag_done, count(t))
                        dve.tensor_scalar(smax[:], neg_smax[:], -1.0, const[:], ALU.mult, ALU.add).then_inc(smax_done, 1)
                    if live(t - 2):
                        mean_var(1, t - 2, r3_stats_done, r3_mean_done, r3_var_done)

                    def out_shift():
                        if live(t - 2):
                            dve.wait_ge(rstd3_done, count(t - 2))
                            if begun(t - 3):
                                dve.wait_ge(y3_done, count(t - 3))
                            dve.scalar_tensor_tensor(shift[1][:], mv[1][:, :, 0], -1.0, rstd[1][:], ALU.mult, ALU.mult)\
                                .then_inc(r3_shift_done, 1)

                    def sum_inverse():
                        if live(t + 1):
                            dve.wait_ge(a_exp_done, count(t + 1))
                            dve.reciprocal(sinv[:], ssum[:]).then_inc(sinv_done, 1)

                    def normalise():
                        if live(t + 1):
                            dve.wait_ge(sinv_done, count(t + 1))
                            dve.tensor_tensor(a_sb[:], a_sb[:], sinv[:].unsqueeze(2).broadcast_to([P, CT, NQ]),
                                              ALU.mult).then_inc(a_done, 1)

                    def token_max():
                        if live(t + 1):
                            dve.wait_ge(maxrow_done, count(t + 1))
                            if begun(t):
                                dve.wait_ge(b_exp_done, count(t))
                            dve.tensor_reduce(neg_m[:], bc_ps, AX.X, ALU.max, negate=True).then_inc(neg_m_done, 1)

                    def z_stats():
                        if live(t):
                            dve.wait_ge(z_done[0], count(t))
                            dve.bn_stats(st[0][:, 0, :], z_ps[0])

                    if live(t - 1):
                        leaves(t - 1, {1: sum_inverse, 2: normalise, 3: out_shift, 6: z_stats, 7: token_max})
                    else:
                        sum_inverse()
                        normalise()
                        out_shift()
                        z_stats()
                        token_max()
                    if live(t + 1):
                        dve.wait_ge(b_exp_done, count(t + 1))
                        for k in range(KT):
                            ins = dve.tensor_tensor_reduce(scratch[:, k, :], c[v_][:, k, :], eb[:], 1.0, 0.0, ALU.mult,
                                                           ALU.add, q2_raw[:, k:k + 1])
                        ins.then_inc(q2_sum_done, 1)
                        dve.reciprocal(ebinv[:], ebsum[:]).then_inc(eb_inv_done, 1)
                    if live(t):
                        dve.wait_ge(z_done[1], count(t))
                        dve.bn_stats(st[0][:, 1, :], z_ps[1]).then_inc(z_stats_done, 1)
                    if live(t + 1):
                        dve.wait_ge(eb_inv_done, count(t + 1))
                        dve.wait_ge(q2_sum_done, count(t + 1))
                        dve.tensor_scalar(q2[:], q2_raw[:], ebinv[:], None, ALU.mult).then_inc(q2_done, 1)
                    if live(t):
                        mean_var(0, t, z_stats_done, z_mean_done, z_var_done)
                    if live(t - 1):
                        dve.wait_ge(lT_hi_done, count(t - 1))
                        dve.tensor_tensor(lT_lo[:], turned_ps[:], f(lT_hi[:]), ALU.subtract).then_inc(lT_lo_done, 1)
                    if live(t):
                        dve.wait_ge(rstd2_done, count(t))
                        if begun(t - 1):
                            dve.wait_ge(y2_done, count(t - 1))
                        dve.scalar_tensor_tensor(shift[0][:], mv[0][:, :, 0], -1.0, rstd[0][:], ALU.mult, ALU.mult)\
                            .then_inc(z_shift_done, 1)
                    if live(t + 1):
                        dve.wait_ge(q2_done, count(t + 1))
                        if begun(t):
                            dve.wait_ge(we_lo_done, count(t))
                        for k in range(KT):
                            ins = dve.scalar_tensor_tensor(we32[:, k, :], wl_raw[:, 3, k, :], q2[:, k:k + 1],
                                                           w1_id[:, k, :], ALU.mult, ALU.add)
                        ins.then_inc(we_done, 1)
                        dve.wait_ge(u_hi_done, count(t + 1))
                        if begun(t):
                            dve.wait_ge(w_lo_done, count(t))
                        dve.tensor_tensor(w32[:], c2q_ps[:], c[v_][:], ALU.mult).then_inc(w_done, 1)
                    if live(t + 1):
                        dve.tensor_tensor(u_r[v_][1][:], c2q_ps[:], f(u_r[v_][0][:]), ALU.subtract).then_inc(u_lo_done, 1)
                    if live(t - 1):
                        dve.wait_ge(tree_done, count(t - 1))
                        if begun(t - 2):
                            dve.wait_ge(y3_done, count(t - 2))
                        dve.tensor_tensor(r3[:], out_ps[:], y2[v_][:], ALU.add).then_inc(res3_done, 1)
                    if live(t):
                        dve.wait_ge(y2T_hi_done, count(t))
                        dve.tensor_tensor(y2T_lo[:], turned_ps[:], f(y2T_hi[:]), ALU.subtract).then_inc(y2T_lo_done, 1)

                steps(dve, step)

            @block.gpsimd
            def _(pool):
                def step(t, u, pair):
                    v_ = 1 - u
                    if live(t - 2):
                        pool.wait_ge(r3_var_done, count(t - 2))
                        if begun(t - 3):
                            pool.wait_ge(y3_done, count(t - 3))
                        pool.tensor_tensor(rstd[1][:], veps[1][:], neg_half[:], ALU.pow).then_inc(rstd3_done, 1)
                    if live(t + 1):
                        pool.wait_ge(c_hi_done, count(t + 1))
                        pool.tensor_tensor(c_r[v_][1][:], c[v_][:], f(c_r[v_][0][:]), ALU.subtract).then_inc(c_lo_done, 1)
                    if live(t):
                        pool.wait_ge(z_var_done, count(t))
                        if begun(t - 1):
                            pool.wait_ge(y2_done, count(t - 1))
                        pool.tensor_tensor(rstd[0][:], veps[0][:], neg_half[:], ALU.pow).then_inc(rstd2_done, 1)
                    if live(t + 1):
                        pool.wait_ge(we_hi_done, count(t + 1))
                        pool.tensor_tensor(we_r[v_][1][:], we32[:], f(we_r[v_][0][:]), ALU.subtract)\
                            .then_inc(we_lo_done, 1)
                        pool.wait_ge(w_hi_done, count(t + 1))
                        pool.tensor_tensor(w_r[v_][1][:], w32[:], f(w_r[v_][0][:]), ALU.subtract).then_inc(w_lo_done, 1)

                steps(pool, step)


_INS = ["x", "ctx_1024", "L0_attn_Wq", "L0_attn_Wkv", "L0_attn_Wo", "L0_xattn_w_cq", "L0_xattn_b_cq", "L0_xattn_w_c",
        "L0_xattn_b_c", "L0_xattn_w_q", "L0_xattn_b_q", "L0_xattn_W_l", "L0_xattn_b_l", "L0_ffn_Wq",
        "L0_ffn_routers", "L0_ffn_leaf_values", "L0_ffn_Wout_w", "L0_ffn_Wout_b"]
_TRANSPOSED = ("L0_xattn_W_l", "L0_ffn_routers", "L0_ffn_leaf_values", "L0_ffn_Wout_w")


def kernel(**inputs):
    import numpy as _np
    import concourse.bacc as _bacc
    from concourse import mybir as _mybir
    from concourse.bass_utils import run_bass_kernel_spmd as _run

    nc = _bacc.Bacc("TRN2", target_bir_lowering=False, num_devices=1)
    arrays, args = {}, []
    for name in _INS:
        a = _np.asarray(inputs[name])
        if name in _TRANSPOSED:
            a = a.T
        if a.ndim == 0:
            a = a.reshape(1)
        a = _np.ascontiguousarray(a)
        arrays[f"in_{name}_dram"] = a
        args.append(nc.dram_tensor(f"in_{name}_dram", a.shape, _mybir.dt.from_np(a.dtype), kind="ExternalInput").ap())
    res = nc.dram_tensor("out_0_dram", (L, NB, D), F32, kind="ExternalOutput").ap()
    decoder_layer(nc, *args, res)
    r = _run(nc, [arrays], core_ids=[0])
    return r.results[0]["out_0_dram"]
```

```python
from contextlib import ExitStack

import concourse.bass as bass
from concourse import mybir

F32 = mybir.dt.float32
F32R = mybir.dt.float32r
ALU = mybir.AluOpType
ACT = mybir.ActivationFunctionType
AX = mybir.AxisListType

P = 128
L = 32
NB = 256
D = 256
KT = D // P
NH = 16
DH = 64
HD = NH * DH
HC = HD // P
GB = P // L
SGT = 2
TOK = SGT * P
NSG = L * NB // TOK
NPROJ = 12
NQ = 77
LEAVES = 256
DEPTH = 8
EPS = 1e-5
SCORE_SCALE = DH ** -0.5
NX = SGT * GB
LO_ROW = 32


def above_zero(value):
    return not isinstance(value, int) or value > 0


def begun(b):
    return not isinstance(b, int) or b >= 0


def live(b):
    return not isinstance(b, int) or 0 <= b < L


def count(b):
    return min(b + 1, L) if isinstance(b, int) else b + 1


def f(ap):
    return ap.bitcast(F32)


def decoder_layer(nc, x, ctx_in, Wq, Wkv, Wo, w_cq, b_cq, w_c, b_c, w_q, b_q, WlT, b_l, fWq, routersT, leafT,
                  WoutT, Wout_b, out):
    with ExitStack() as top:
        def sem(name):
            return top.enter_context(nc.semaphore(name))

        yT = top.enter_context(nc.sbuf_tensor("yT", [P, KT, L * NB], F32))
        ident = top.enter_context(nc.sbuf_tensor("ident", [P, P], F32))
        neg_half = top.enter_context(nc.sbuf_tensor("neg_half", [P, 2], F32))
        s_ident0, s_ident = sem("ident_zeroed"), sem("ident_ready")
        qT_even = top.enter_context(nc.sbuf_tensor("qT0", [P, HC, TOK], F32))
        kT_even = top.enter_context(nc.sbuf_tensor("kT0", [P, HC, TOK], F32))
        cross_w = {"wl": qT_even[:].rearrange("p (f k) e -> p f k e", f=4)}
        for n, name in enumerate(("fwq", "routers", "leaf_v", "wout")):
            cross_w[name] = kT_even[:, n * KT:(n + 1) * KT, :]
        cross_src = {"wl": WlT.rearrange("(f k p) e -> p f k e", f=4, p=P)}
        for name, src in (("fwq", fWq), ("routers", routersT), ("leaf_v", leafT), ("wout", WoutT)):
            cross_src[name] = src.rearrange("(k p) e -> p k e", p=P)
        cross_in = sem("cross_weights_in")
        attention(nc, sem, x, Wq, Wkv, Wo, yT, ident, neg_half, s_ident0, s_ident, qT_even, kT_even, cross_w, cross_src,
                  cross_in)
        cross_and_tree(nc, sem, ctx_in, w_cq, b_cq, w_c, b_c, w_q, b_q, b_l, Wout_b, yT, ident, neg_half, s_ident,
                       cross_w, cross_in, out)


def attention(nc, sem, x, Wq, Wkv, Wo, yT, ident, neg_half, s_ident0, s_ident, qT_even, kT_even, cross_w, cross_src,
                  cross_in):
    with ExitStack() as ctx:
        def sb(name, shape, dt=F32):
            return ctx.enter_context(nc.sbuf_tensor(name, shape, dt))

        w_hi = sb("w_hi", [P, 3, KT, HD], F32R)
        w_lo = sb("w_lo", [P, 3, KT, HD], F32R)
        wo_hi = sb("wo_hi", [P, HC, D], F32R)
        wo_lo = sb("wo_lo", [P, HC, D], F32R)
        xT_hi = sb("xT_hi", [P, KT, TOK], F32R)
        xT_lo = sb("xT_lo", [P, KT, TOK], F32R)
        x_nat = [sb(f"x_nat{u}", [P, SGT, D]) for u in range(2)]
        qT = [qT_even, sb("qT1", [P, HC, TOK])]
        kT = [kT_even, sb("kT1", [P, HC, TOK])]
        v = [sb(f"v{u}", [P, SGT, HD]) for u in range(2)]
        prob = sb("prob", [P, NH, L])
        prob4 = prob[:].rearrange("p (r n) j -> p r n j", r=2)
        probT = sb("probT", [P, NH, P])
        rowmax = sb("rowmax", [P, NH])
        rowsum = sb("rowsum", [P, NH])
        rowinv = sb("rowinv", [P, NH])
        vecT_hi = sb("vecT_hi", [P, HC, P], F32R)
        vecT_lo = sb("vecT_lo", [P, HC, P], F32R)
        x_res = [sb(f"x_res{g}", [P, D]) for g in range(SGT)]
        res = sb("res", [P, D])
        y_nat = sb("y_nat", [P, D])
        stats = sb("stats", [P, 6])
        mv = sb("mv", [P, 2])
        veps = sb("veps", [P, 1])
        rstd = sb("rstd", [P, 1])

        NCH = 8
        w_in = [sem(f"w_in{n}") for n in range(NCH)]
        w_hi_done, w_lo_done, zeroed = sem("weights_hi_done"), sem("weights_lo_done"), sem("constants_ready")

        def chunk(n):
            j, h = n // 2, n % 2
            half = slice(h * 512, (h + 1) * 512)
            staged = yT[:, 0, n * 1024:(n + 1) * 1024]
            if j < 3:
                src = (Wq, Wkv[:, 0:HD], Wkv[:, HD:2 * HD])[j][:, half].rearrange("(k p) n -> p k n", p=P)
                return (src, staged.rearrange("p (k n) -> p k n", k=KT), w_hi[:, j, :, half], w_lo[:, j, :, half])
            rows = slice(h * HC // 2, (h + 1) * HC // 2)
            return (Wo[half, :].rearrange("(c p) n -> p c n", p=P), staged.rearrange("p (c n) -> p c n", n=D),
                    wo_hi[:, rows, :], wo_lo[:, rows, :])

        def ps(name, shape):
            return ctx.enter_context(nc.psum_tensor(name, shape, F32))

        xT_ps = ps("xT_ps", [P, KT, TOK])
        proj_ps = [ps(f"proj_ps{u}", [P, 512]) for u in range(2)]
        score_ps = ps("score_ps", [P, 2, 512])
        s_view = score_ps[:, :, 0:NH // 2 * L].rearrange("p r (n j) -> p r n j", j=L)
        vecT_ps = ps("vecT_ps", [P, HC, P])
        oy_ps = ps("oy_ps", [P, 2, D])
        o_ps = oy_ps[:, 0, :]
        yT_ps = oy_ps[:, 1, :].rearrange("p (k t) -> p k t", k=KT)

        x_in = [sem(f"x_in{u}") for u in range(2)]
        res_in = [sem(f"res_in{g}") for g in range(SGT)]
        xT_done, xhi_done, xlo_done = sem("xT_done"), sem("xhi_done"), sem("xlo_done")
        proj_done, evac_act, evac_dve = sem("proj_done"), sem("evac_act"), sem("evac_dve")
        score_done, max_done, sub_done, exp_done = sem("score_done"), sem("max_done"), sem("sub_done"), sem("exp_done")
        sum_done, inv_done, prob_done, probT_done = sem("sum_done"), sem("inv_done"), sem("prob_done"), sem("probT_done")
        pv_done, vhi_done, vlo_done, o_done = sem("pv_done"), sem("vhi_done"), sem("vlo_done"), sem("o_done")
        res_done, st_done, mv_done, eps_done = sem("res_done"), sem("st_done"), sem("mv_done"), sem("eps_done")
        rstd_done, y_done, ytr_done, yT_done = sem("rstd_done"), sem("y_done"), sem("ytr_done"), sem("yT_done")

        def steps(eng, step):
            step(0, 0, 0, 2)
            step(1, 1, 0, 2)
            with eng.Fori(1, NSG // 2 - 1) as pair:
                step(pair * 2, 0, pair, 2)
                step(pair * 2 + 1, 1, pair, 2)
            step(NSG - 2, 0, NSG // 2 - 1, 1)
            step(NSG - 1, 1, NSG // 2 - 1, 0)

        with nc.Block() as block:
            @block.sync
            def _(sp):
                def load(s, u):
                    if above_zero(s - 1):
                        sp.wait_ge(xT_done, s - 1)
                    for g in range(SGT):
                        columns(x_nat[u][:, g, :], s, g, x_in[u])

                def columns(dst, s, g, landed):
                    for b in range(GB):
                        col = s * (SGT * GB) + (g * GB + b)
                        sp.dma_start(dst[b * L:(b + 1) * L, :], x[:, bass.ds(col, 1), :].rearrange(
                            "i a d -> i (a d)")).then_inc(landed, 16)

                def load_res(s):
                    for g in range(SGT):
                        if above_zero((s - 1) * SGT + g + 1):
                            sp.wait_ge(res_done, (s - 1) * SGT + g + 1)
                        columns(x_res[g], s, g, res_in[g])

                load(0, 0)
                for n in range(1, NCH):
                    sp.dma_start(chunk(n)[1], chunk(n)[0]).then_inc(w_in[n], 16)
                load(1, 1)
                load_res(0)
                load(2, 0)
                load_res(1)
                load(3, 1)
                with sp.Fori(1, NSG // 2 - 1) as pair:
                    load_res(pair * 2)
                    load(pair * 2 + 2, 0)
                    load_res(pair * 2 + 1)
                    load(pair * 2 + 3, 1)
                load_res(NSG - 2)
                load_res(NSG - 1)
                sp.wait_ge(score_done, (NSG - 1) * SGT)
                for name, dst in cross_w.items():
                    src = cross_src[name]
                    sp.dma_start(dst[:, :, 0:src.shape[2]] if name == "routers" else dst, src).then_inc(cross_in, 16)

            @block.tensor
            def _(pe):
                def xtr(u, turn):
                    pe.wait_ge(x_in[u], turn * (16 * NX) + 16 * NX)
                    for k in range(KT):
                        for g in range(SGT):
                            ins = pe.transpose(xT_ps[:, k, g * P:(g + 1) * P], x_nat[u][:, g, k * P:(k + 1) * P],
                                               ident[:])
                    ins.then_inc(xT_done, 1)

                def proj(s, j):
                    if j == 0:
                        pe.wait_ge(xhi_done, s + 1)
                        pe.wait_ge(xlo_done, s + 1)
                    if above_zero(s * (NPROJ // 2) + j // 2):
                        pe.wait_ge(evac_dve if j % 2 else evac_act, s * (NPROJ // 2) + j // 2)
                    bank = proj_ps[j % 2]
                    if j < 8:
                        for h in range(2):
                            c = (2 * j + h) % HC
                            m = 0
                            for k in range(KT):
                                for w, t in ((w_hi, xT_hi), (w_hi, xT_lo), (w_lo, xT_hi)):
                                    ins = pe.matmul(bank[:, h * TOK:(h + 1) * TOK], w[:, j // 4, k, c * P:(c + 1) * P],
                                                    t[:, k, :], start=(m == 0), stop=(m == 5))
                                    m += 1
                    else:
                        g, h = (j - 8) // 2, (j - 8) % 2
                        m = 0
                        for k in range(KT):
                            for t, w in ((xT_hi, w_hi), (xT_hi, w_lo), (xT_lo, w_hi)):
                                ins = pe.matmul(bank[:], t[:, k, g * P:(g + 1) * P], w[:, 2, k, h * 512:(h + 1) * 512],
                                                start=(m == 0), stop=(m == 5))
                                m += 1
                    ins.then_inc(proj_done, 1)

                def scores(T, u, g):
                    if g:
                        pe.wait_ge(s_ident, 1)
                        if above_zero(T):
                            pe.wait_ge(sub_done, T)
                    for n in range(NH):
                        r = (n % 2) * DH
                        for b in range(GB):
                            t0 = g * P + b * L
                            ins = pe.matmul(s_view[b * L:(b + 1) * L, n % 2, n // 2, :], qT[u][r:r + DH, n // 2, t0:t0 + L],
                                            kT[u][r:r + DH, n // 2, t0:t0 + L], start=True, stop=True)
                    ins.then_inc(score_done, 1)

                def context(T, u, g):
                    pe.wait_ge(probT_done, T + 1)
                    if above_zero(T):
                        pe.wait_ge(vlo_done, T)
                    for n in range(NH):
                        r = (n % 2) * DH
                        ins = pe.matmul(vecT_ps[r:r + DH, n // 2, :], v[u][:, g, n * DH:(n + 1) * DH], probT[:, n % 2 * (NH // 2) + n // 2, :],
                                        start=True, stop=True)
                    ins.then_inc(pv_done, 1)

                def project_out(T):
                    pe.wait_ge(vlo_done, T + 1)
                    if isinstance(T, int) and T == 0:
                        pe.wait_ge(w_lo_done, NCH)
                    if above_zero(T):
                        pe.wait_ge(res_done, T)
                    if above_zero(T):
                        pe.wait_ge(yT_done, T)
                    m = 0
                    for c in range(HC):
                        for t, w in ((vecT_hi, wo_hi), (vecT_hi, wo_lo), (vecT_lo, wo_hi)):
                            ins = pe.matmul(o_ps, t[:, c, :], w[:, c, :], start=(m == 0), stop=(m == 3 * HC - 1))
                            m += 1
                    ins.then_inc(o_done, 1)

                def ytr(T):
                    pe.wait_ge(y_done, T + 1)
                    if above_zero(T):
                        pe.wait_ge(yT_done, T)
                    for k in range(KT):
                        ins = pe.transpose(yT_ps[:, k, :], y_nat[:, k * P:(k + 1) * P], ident[:])
                    ins.then_inc(ytr_done, 1)

                def step(s, u, pair, ahead):
                    nxt = s + 1
                    for g in range(SGT):
                        T = s * SGT + g
                        if ahead or g == 0:
                            scores(T, u, g)
                        if ahead:
                            for j in range(6 * g, 6 * g + 4):
                                proj(nxt, j)
                        if above_zero(T):
                            project_out(T - 1)
                        if ahead:
                            for j in range(6 * g + 4, 6 * g + 6):
                                proj(nxt, j)
                        elif g == 0:
                            scores(T + 1, u, 1)
                        context(T, u, g)
                        if above_zero(T):
                            ytr(T - 1)
                    if ahead:
                        pe.wait_ge(evac_act, (s + 2) * (NPROJ // 2))
                        pe.wait_ge(evac_dve, (s + 2) * (NPROJ // 2))
                        pe.wait_ge(sub_done, s * SGT + SGT)
                    if ahead == 2:
                        xtr(u, pair + 1)

                pe.wait_ge(s_ident, 1)
                xtr(0, 0)
                for j in range(NPROJ):
                    pe.wait_ge(w_lo_done, j // 2 + 1 if j < 9 else 6)
                    proj(0, j)
                pe.wait_ge(evac_act, NPROJ // 2)
                pe.wait_ge(evac_dve, NPROJ // 2)
                xtr(1, 0)
                steps(pe, step)
                project_out(2 * NSG - 1)
                ytr(2 * NSG - 1)

            def evacuated_to(s_parity, j):
                if j < 8:
                    dst = (qT, kT)[j // 4][s_parity]
                    return dst[:, 2 * (j % 4):2 * (j % 4) + 2, :].rearrange("p c t -> p (c t)")
                g, h = (j - 8) // 2, (j - 8) % 2
                return v[s_parity][:, g, h * 512:(h + 1) * 512]

            @block.scalar
            def _(act):
                def xhi(s):
                    act.wait_ge(xT_done, s + 1)
                    if above_zero(s * NPROJ):
                        act.wait_ge(proj_done, s * NPROJ)
                    act.activation(xT_hi[:], xT_ps[:], ACT.Copy).then_inc(xhi_done, 1)

                def evac(s, u, j):
                    act.wait_ge(proj_done, s * NPROJ + (j + 1))
                    act.activation(evacuated_to(u, j), proj_ps[0][:], ACT.Copy).then_inc(evac_act, 1)

                def yT_copy(T):
                    act.wait_ge(ytr_done, T + 1)
                    dst = yT[:].rearrange("p k (i b) -> p k i b", i=L)
                    for k in range(KT):
                        act.activation(dst[:, k, :, bass.ds(T * GB, GB)],
                                       yT_ps[:, k, :].rearrange("p (b i) -> p i b", b=GB),
                                       ACT.Copy).then_inc(yT_done, 1) if k == KT - 1 else \
                            act.activation(dst[:, k, :, bass.ds(T * GB, GB)],
                                           yT_ps[:, k, :].rearrange("p (b i) -> p i b", b=GB), ACT.Copy)

                def step(s, u, pair, ahead):
                    for g in range(SGT):
                        T = s * SGT + g
                        act.wait_ge(sub_done, T + 1)
                        act.activation(prob[:], prob[:], ACT.Exp, scale=SCORE_SCALE).then_inc(exp_done, 1)
                        if ahead:
                            evac(s + 1, 1 - u, 6 * g)
                            evac(s + 1, 1 - u, 6 * g + 2)
                            evac(s + 1, 1 - u, 6 * g + 4)
                        act.wait_ge(pv_done, T + 1)
                        if above_zero(T):
                            act.wait_ge(o_done, T)
                        act.activation(vecT_hi[:], vecT_ps[:], ACT.Copy).then_inc(vhi_done, 1)
                        if above_zero(T):
                            yT_copy(T - 1)
                    if ahead == 2:
                        xhi(s + 2)

                def weights_hi(n):
                    act.wait_ge(w_in[n], 16)
                    act.activation(chunk(n)[2], chunk(n)[1], ACT.Copy).then_inc(w_hi_done, 1)

                act.dma_start(chunk(0)[1], chunk(0)[0]).then_inc(w_in[0], 16)
                weights_hi(0)
                xhi(0)
                weights_hi(1)
                for j in range(0, NPROJ, 2):
                    weights_hi(2 + j // 2)
                    evac(0, 0, j)
                xhi(1)
                steps(act, step)
                yT_copy(2 * NSG - 1)

            @block.vector
            def _(dve):
                def xlo(s):
                    dve.wait_ge(xhi_done, s + 1)
                    dve.tensor_tensor(xT_lo[:], xT_ps[:], f(xT_hi[:]), ALU.subtract).then_inc(xlo_done, 1)

                def evac(s, u, j):
                    dve.wait_ge(proj_done, s * NPROJ + (j + 1))
                    dve.tensor_copy(evacuated_to(u, j), proj_ps[1][:]).then_inc(evac_dve, 1)

                def norm(s, T, g):
                    dve.wait_ge(res_in[g], (s + 1) * (16 * GB))
                    dve.wait_ge(o_done, T + 1)
                    dve.tensor_tensor(res[:], o_ps, x_res[g][:], ALU.add).then_inc(res_done, 1)
                    dve.wait_ge(res_done, T + 1)
                    dve.bn_stats(stats[:], res[:]).then_inc(st_done, 1)
                    dve.wait_ge(s_ident, 1)
                    dve.wait_ge(st_done, T + 1)
                    dve.bn_aggr(mv[:], stats[:]).then_inc(mv_done, 1)
                    dve.wait_ge(mv_done, T + 1)
                    dve.tensor_scalar(veps[:], mv[:, 1:2], EPS, None, ALU.add).then_inc(eps_done, 1)

                def norm_out(T):
                    dve.wait_ge(rstd_done, T + 1)
                    if above_zero(T):
                        dve.wait_ge(ytr_done, T)
                    dve.tensor_scalar(y_nat[:], res[:], mv[:, 0:1], rstd[:], ALU.subtract, ALU.mult).then_inc(y_done, 1)

                def step(s, u, pair, ahead):
                    for g in range(SGT):
                        T = s * SGT + g
                        dve.wait_ge(score_done, T + 1)
                        dve.tensor_reduce(rowmax[:].rearrange("p (r n) -> p r n", r=2), s_view, AX.X, ALU.max).then_inc(max_done, 1)
                        dve.wait_ge(max_done, T + 1)
                        dve.tensor_tensor(prob4, s_view, rowmax[:].rearrange("p (r n) -> p r n", r=2).unsqueeze(3)
                                          .broadcast_to([P, 2, NH // 2, L]), ALU.subtract).then_inc(sub_done, 1)
                        if ahead:
                            evac(s + 1, 1 - u, 6 * g + 1)
                        dve.wait_ge(exp_done, T + 1)
                        dve.tensor_reduce(rowsum[:], prob[:], AX.X, ALU.add).then_inc(sum_done, 1)
                        dve.wait_ge(sum_done, T + 1)
                        dve.reciprocal(rowinv[:], rowsum[:]).then_inc(inv_done, 1)
                        if ahead:
                            evac(s + 1, 1 - u, 6 * g + 3)
                        dve.wait_ge(prob_done, T + 1)
                        if above_zero(T):
                            dve.wait_ge(pv_done, T)
                        for b in range(GB):
                            ins = dve.transpose(probT[b * L:(b + 1) * L, :, b * L:(b + 1) * L],
                                                prob[b * L:(b + 1) * L, :, :])
                        ins.then_inc(probT_done, 1)
                        if above_zero(T):
                            norm(s - (1 - g), T - 1, 1 - g)
                            norm_out(T - 1)
                        if ahead:
                            evac(s + 1, 1 - u, 6 * g + 5)
                        dve.wait_ge(vhi_done, T + 1)
                        dve.tensor_tensor(vecT_lo[:], vecT_ps[:], f(vecT_hi[:]), ALU.subtract).then_inc(vlo_done, 1)
                    if ahead == 2:
                        xlo(s + 2)

                def weights_lo(n):
                    dve.wait_ge(w_hi_done, n + 1)
                    dve.tensor_tensor(chunk(n)[3], chunk(n)[1], f(chunk(n)[2]), ALU.subtract).then_inc(w_lo_done, 1)

                dve.memset(probT[:], 0.0)
                weights_lo(0)
                xlo(0)
                weights_lo(1)
                for j in range(1, NPROJ, 2):
                    weights_lo(2 + j // 2)
                    evac(0, 0, j)
                xlo(1)
                steps(dve, step)
                norm(NSG - 1, 2 * NSG - 1, 1)
                norm_out(2 * NSG - 1)

            @block.gpsimd
            def _(pool):
                def rstd_of(T):
                    pool.wait_ge(eps_done, T + 1)
                    pool.tensor_tensor(rstd[:], veps[:], neg_half[:, 0:1], ALU.pow).then_inc(rstd_done, 1)

                def step(s, u, pair, ahead):
                    for g in range(SGT):
                        T = s * SGT + g
                        pool.wait_ge(inv_done, T + 1)
                        pool.tensor_tensor(prob[:], prob[:], rowinv[:].unsqueeze(2).broadcast_to([P, NH, L]),
                                           ALU.mult).then_inc(prob_done, 1)
                        if above_zero(T):
                            rstd_of(T - 1)

                pool.memset(ident[:], 0.0).then_inc(s_ident0, 1)
                pool.wait_ge(s_ident0, 1)
                pool.affine_select(out=ident[:], in_=ident[:], compare_op=ALU.not_equal, fill=1.0, base=0,
                                   pattern=[[-1, P]], channel_multiplier=1).then_inc(s_ident, 1)
                pool.memset(neg_half[:], -0.5).then_inc(zeroed, 1)
                pool.wait_ge(zeroed, 1)
                steps(pool, step)
                rstd_of(2 * NSG - 1)


def cross_and_tree(nc, sem, ctx_in, w_cq, b_cq, w_c, b_c, w_q, b_q, b_l, Wout_b, yT, ident, neg_half, s_ident,
                   cross_w, cross_in, out):
    CT = NB // P
    with ExitStack() as ctx:
        def sb(name, shape, dt=F32):
            return ctx.enter_context(nc.sbuf_tensor(name, shape, dt))

        def ps(name, shape):
            return ctx.enter_context(nc.psum_tensor(name, shape, F32))

        def halves(name, shape, n):
            return [(sb(f"{name}_hi{u}", shape, F32R), sb(f"{name}_lo{u}", shape, F32R)) for u in range(n)]

        wl_raw = cross_w["wl"]
        w1_id = sb("w1_id", [P, KT, D])
        [(w2_hi, w2_lo)] = halves("w2", [P, KT, D], 1)
        [(w3_hi, w3_lo)] = halves("w3", [P, KT, D], 1)
        fwq, routers, leaf_v, wout = (cross_w[name] for name in ("fwq", "routers", "leaf_v", "wout"))
        [(gate_hi, gate_lo)] = halves("gate", [P, KT, LEAVES], 1)
        [(leafw_hi, leafw_lo)] = halves("leafw", [P, KT, D], 1)
        vec3 = sb("vec3", [P, 3, KT])
        consts = sb("consts", [P, 3])
        const = sb("const", [P, 1])
        wq_rows = sb("wq_rows", [P, KT, P])
        ones = sb("ones", [P, P])
        ones_r = sb("ones_r", [P, P], F32R)
        bias_raw = sb("bias_raw", [P, 2, D])
        bias_r = sb("bias_r", [P, 2, D], F32R)

        q_nat = [sb(f"q_nat{u}", [NQ, D]) for u in range(2)]
        qT = sb("cqT", [P, KT, NQ])
        g_mat = sb("g_mat", [P, KT, NQ])
        c = [sb(f"c{u}", [P, KT, NB]) for u in range(2)]
        c_r = halves("c", [P, KT, NB], 2)
        u_r = halves("u", [P, KT, NB], 2)
        w_r = halves("w", [P, KT, NB], 2)
        we_r = halves("we", [P, KT, D], 2)
        w32 = sb("w32", [P, KT, NB])
        we32 = sb("we32", [P, KT, D])
        a_sb = sb("a_sb", [P, CT, NQ])
        aT = sb("aT", [NQ, NB])
        neg_smax = sb("neg_smax", [P, CT])
        smax = sb("smax", [P, CT])
        ssum = sb("ssum", [P, CT])
        sinv = sb("sinv", [P, CT])
        diag = sb("diag", [P, CT, P])
        neg_m = sb("neg_m", [P, 1])
        eb = sb("eb", [P, NB])
        ebsum = sb("ebsum", [P, 1])
        ebinv = sb("ebinv", [P, 1])
        scratch = sb("scratch", [P, KT, NB])
        q2_raw = sb("q2_raw", [P, KT])
        q2 = sb("q2", [P, KT])
        y2 = [sb(f"y2_{u}", [P, CT, D]) for u in range(2)]
        [(y2T_hi, y2T_lo)] = halves("y2T", [P, KT, NB], 1)
        th = sb("th", [P, CT, LEAVES])
        lv = [sb(f"lv{u}", [P, CT, LEAVES // 2]) for u in range(2)]
        leaf = sb("leaf", [P, CT, LEAVES])
        [(lT_hi, lT_lo)] = halves("lT", [P, KT, NB], 1)
        r3 = [sb(f"r3_{u}", [P, CT, D]) for u in range(2)]
        y3 = [sb(f"y3_{u}", [P, CT, D]) for u in range(2)]
        st = [sb(f"st{n}", [P, CT, 6]) for n in range(3)]
        mv = [sb(f"mv{n}", [P, CT, 2]) for n in range(3)]
        veps = [sb(f"veps{n}", [P, CT]) for n in range(3)]
        rstd = [sb(f"rstd{n}", [P, CT]) for n in range(3)]
        shift = sb("shift", [P, CT])

        s_bank = ps("s_ps", [P, 512])
        out_ps = ps("out_ps", [P, CT, D])
        turned_ps = ps("turned_ps", [P, KT, NB])
        z_bank = [ps(f"z_ps{ct}", [P, 512]) for ct in range(CT)]
        z_ps = [bank[:, 0:D] for bank in z_bank]
        aq_ps = ps("aq_ps", [P, 512])
        c2q_ps = ps("c2q_ps", [P, KT, NB])
        gate_bc_ps = ps("gate_bc_ps", [P, 512])
        gate_ps = gate_bc_ps[:].rearrange("p (c n) -> p c n", c=CT)
        bc_ps = gate_bc_ps[:, 0:NB]
        s_ps = s_bank[:, 0:CT * NQ].rearrange("p (c q) -> p c q", c=CT)
        aT_ps = aq_ps[:, 0:NB]
        qT_ps = aq_ps[:, NB:NB + KT * NQ].rearrange("p (k q) -> p k q", k=KT)

        ld, fused, setup = sem("c_loaded"), sem("c_fused"), sem("c_setup")
        highs = sem("c_high_halves")
        setup_v = [0]
        q_in = [sem(f"q_in{u}") for u in range(2)]
        c_in = [sem(f"c_in{u}") for u in range(2)]
        NLOADS = 10
        with nc.allow_non_contiguous_dma("small vectors"), nc.Block() as block:
            @block.sync
            def _(sp):
                for n, w in enumerate((w_cq, w_c, w_q)):
                    sp.dma_start(vec3[:, n, :], w.rearrange("(k p) -> p k", p=P)).then_inc(ld, 16)
                for n, b in enumerate((b_cq, b_c, b_q)):
                    sp.dma_start(consts[:, n:n + 1], b.partition_broadcast(P)).then_inc(ld, 16)
                for b in range(2):
                    sp.dma_start(q_nat[b][:], ctx_in[b, :, :]).then_inc(q_in[b], 16)
                    sp.dma_start(c[b][:], yT[:, :, b * NB:(b + 1) * NB]).then_inc(c_in[b], 16)
                sp.wait_ge(setup, 1)
                for row in (0, LO_ROW):
                    for n, b in enumerate((b_l, Wout_b)):
                        sp.dma_start(bias_raw[row:row + 1, n, :], b.rearrange("(a e) -> a e", a=1)).then_inc(ld, 16)

            @block.tensor
            def _(pe):
                pe.wait_ge(cross_in, 16 * len(cross_w))
                pe.wait_ge(setup, 2)
                for k in range(KT):
                    for e in range(KT):
                        ins = pe.matmul(z_ps[k], fwq[:, e, k * P:(k + 1) * P], routers[:, e, :], start=(e == 0),
                                        stop=(e == KT - 1))
                ins.then_inc(fused, 1)
                for k in range(KT):
                    for e in range(KT):
                        ins = pe.matmul(c2q_ps[:, k, :], leaf_v[:, e, k * P:(k + 1) * P], wout[:, e, :],
                                        start=(e == 0), stop=(e == KT - 1))
                ins.then_inc(fused, 1)

            @block.scalar
            def _(act):
                act.wait_ge(cross_in, 16 * len(cross_w))
                act.activation(w2_hi[:], wl_raw[:, 1], ACT.Copy).then_inc(highs, 1)
                act.activation(w3_hi[:], wl_raw[:, 2], ACT.Copy).then_inc(highs, 1)
                act.wait_ge(fused, 1)
                for k in range(KT):
                    ins = act.activation(gate_hi[:, k, :], z_ps[k], ACT.Copy)
                ins.then_inc(highs, 1)
                act.wait_ge(fused, 2)
                act.activation(leafw_hi[:], c2q_ps[:], ACT.Copy, scale=2.0 ** -DEPTH).then_inc(highs, 1)

            @block.vector
            def _(dve):
                def chain(ins):
                    setup_v[0] += 1
                    ins.then_inc(setup, 1)
                    dve.wait_ge(setup, setup_v[0])

                chain(dve.memset(bias_raw[:], 0.0))
                dve.wait_ge(cross_in, 16 * len(cross_w))
                chain(dve.memset(routers[:, :, LEAVES - 1:LEAVES], 0.0))
                dve.wait_ge(cross_in, 16 * len(cross_w))
                chain(dve.memset(ones[:], 1.0))
                chain(dve.tensor_copy(ones_r[:], ones[:]))
                chain(dve.tensor_copy(w1_id[:], wl_raw[:, 0]))
                for k in range(KT):
                    part = w1_id[:, k, k * P:(k + 1) * P]
                    chain(dve.tensor_tensor(part, part, ident[:], ALU.add))
                dve.wait_ge(highs, 1)
                dve.tensor_tensor(w2_lo[:], wl_raw[:, 1], f(w2_hi[:]), ALU.subtract)
                dve.wait_ge(highs, 2)
                dve.tensor_tensor(w3_lo[:], wl_raw[:, 2], f(w3_hi[:]), ALU.subtract)
                dve.wait_ge(ld, 16 * NLOADS)
                for k in range(KT):
                    chain(dve.tensor_scalar(wq_rows[:, k, :], ones[:], vec3[:, 2, k:k + 1], None, ALU.mult))
                chain(dve.tensor_tensor(const[:], consts[:, 0:1], consts[:, 1:2], ALU.add))
                chain(dve.tensor_tensor(const[:], const[:], consts[:, 2:3], ALU.add))
                chain(dve.tensor_copy(bias_r[:], bias_raw[:]))
                low = slice(LO_ROW, LO_ROW + 1)
                chain(dve.tensor_tensor(bias_r[low], bias_raw[low], f(bias_r[low]), ALU.subtract))
                dve.wait_ge(highs, 3)
                for k in range(KT):
                    dve.tensor_tensor(gate_lo[:, k, :], z_ps[k], f(gate_hi[:, k, :]), ALU.subtract)
                dve.wait_ge(highs, 4)
                dve.scalar_tensor_tensor(leafw_lo[:], c2q_ps[:], 2.0 ** -DEPTH, f(leafw_hi[:]), ALU.mult, ALU.subtract)

        gate_done = sem("gate_done")
        scores_done = sem("scores_done")
        z_done = [sem(f"z_done{ct}") for ct in range(CT)]
        maxrow_done = sem("maxrow_done")
        aTr_done = sem("aTr_done")
        leafTr_done = sem("leafTr_done")
        c2q_done = sem("c2q_done")
        y2Tr_done = sem("y2Tr_done")
        qTr_done = sem("qTr_done")
        tree_done = sem("tree_done")
        tanh_done = sem("tanh_done")
        a_exp_done = sem("a_exp_done")
        b_exp_done = sem("b_exp_done")
        aT_copied = sem("aT_copied")
        lT_hi_done = sem("lT_hi_done")
        we_hi_done = sem("we_hi_done")
        u_hi_done = sem("u_hi_done")
        w_hi_done = sem("w_hi_done")
        y2T_hi_done = sem("y2T_hi_done")
        g_mat_done = sem("g_mat_done")
        c_hi_done = sem("c_hi_done")
        neg_smax_done = sem("neg_smax_done")
        smax_done = sem("smax_done")
        diag_done = sem("diag_done")
        sinv_done = sem("sinv_done")
        a_done = sem("a_done")
        z_stats_done = sem("z_stats_done")
        z_mean_done = sem("z_mean_done")
        z_var_done = sem("z_var_done")
        z_shift_done = sem("z_shift_done")
        y2_done = [sem(f"y2_done{ct}") for ct in range(CT)]
        neg_m_done = sem("neg_m_done")
        q2_sum_done = sem("q2_sum_done")
        eb_inv_done = sem("eb_inv_done")
        q2_done = sem("q2_done")
        we_done = sem("we_done")
        u_lo_done = sem("u_lo_done")
        w_done = sem("w_done")
        lT_lo_done = sem("lT_lo_done")
        y2T_lo_done = sem("y2T_lo_done")
        qT_copied = sem("qT_copied")
        c_lo_done = sem("c_lo_done")
        res3_done = sem("res3_done")
        r3_stats_done = sem("r3_stats_done")
        r3_mean_done = sem("r3_mean_done")
        r3_var_done = sem("r3_var_done")
        leaves_done = sem("leaves_done")
        rstd2_done = sem("rstd2_done")
        we_lo_done = sem("we_lo_done")
        w_lo_done = sem("w_lo_done")
        rstd3_done = sem("rstd3_done")
        y3_done = sem("y3_done")
        level_done = sem("level_done")
        y_out = [sem(f"y_out{u}") for u in range(2)]
        NLV = DEPTH - 1

        def steps(eng, step):
            for t in range(-2, 4):
                step(t, t % 2, t // 2)
            with eng.Fori(2, L // 2 - 1) as pair:
                step(pair * 2, 0, pair)
                step(pair * 2 + 1, 1, pair)
            for t in range(L - 2, L + 2):
                step(t, t % 2, t // 2)

        with nc.Block() as block:
            @block.sync
            def _(sp):
                def load(b, u):
                    if begun(b - 2):
                        sp.wait_ge(c2q_done, count(b - 2))
                    sp.dma_start(q_nat[u][:], ctx_in[bass.ds(b, 1), :, :].rearrange("a q d -> (a q) d"))\
                        .then_inc(q_in[u], 16)

                def load_c(b, u):
                    if begun(b - 2):
                        sp.wait_ge(scores_done, count(b - 2))
                    if begun(b - 2):
                        sp.wait_ge(c_lo_done, count(b - 2))
                    if begun(b - 2):
                        sp.wait_ge(q2_sum_done, count(b - 2))
                    if begun(b - 2):
                        sp.wait_ge(w_done, count(b - 2))
                    sp.dma_start(c[u][:], yT[:, :, bass.ds(b * NB, NB)]).then_inc(c_in[u], 16)

                def store(b, u):
                    sp.wait_ge(y3_done, count(b))
                    for ct in range(CT):
                        sp.dma_start(out[bass.ds(b, 1), ct * P:(ct + 1) * P, :].rearrange("a c d -> (a c) d"),
                                     y3[u][:, ct, :]).then_inc(y_out[u], 16)

                def step(t, u, pair):
                    if begun(t) and live(t + 2):
                        load_c(t + 2, u)
                    if live(t - 3):
                        store(t - 3, 1 - u)
                    if begun(t + 1) and live(t + 3):
                        load(t + 3, 1 - u)

                for t in range(-2, 4):
                    step(t, t % 2, t // 2)
                with sp.Fori(2, L // 2 - 2) as pair:
                    step(pair * 2, 0, pair)
                    step(pair * 2 + 1, 1, pair)
                for t in range(L - 4, L + 3):
                    step(t, t % 2, t // 2)
                for u in range(2):
                    sp.wait_ge(y_out[u], 16 * CT * (L // 2))

            @block.tensor
            def _(pe):
                def three(dst, lt, rt, first, last):
                    m = 0
                    for k in range(KT):
                        for a, b in ((0, 0), (0, 1), (1, 0)):
                            ins = pe.matmul(dst, lt(a, k), rt(b, k), start=(first and m == 0),
                                            stop=(last and m == 3 * KT - 1))
                            m += 1
                    return ins

                def add_bias(dst, n):
                    return pe.matmul(dst, ones_r[:], bias_r[:, n, :], start=False, stop=True)

                def step(t, u, pair):
                    v_ = 1 - u
                    if live(t - 1):
                        pe.wait_ge(y2T_hi_done, count(t - 1))
                        pe.wait_ge(y2T_lo_done, count(t - 1))
                        if live(t):
                            pe.wait_ge(b_exp_done, count(t))
                        for ct in range(CT):
                            ins = three(gate_ps[:, ct, :], lambda a, k: (y2T_hi, y2T_lo)[a][:, k, ct * P:(ct + 1) * P],
                                        lambda b, k: (gate_hi, gate_lo)[b][:, k, :], True, True)
                        ins.then_inc(gate_done, 1)

                    def project_c2q(ct):
                        if ct == 0:
                            pe.wait_ge(u_hi_done, count(t))
                            pe.wait_ge(u_lo_done, count(t))
                            if begun(t - 1):
                                pe.wait_ge(y2_done[1], count(t - 1))
                        three(z_ps[ct], lambda a, k: u_r[u][a][:, k, ct * P:(ct + 1) * P],
                              lambda b, k: (w2_hi, w2_lo)[b][:, k, :], True, False)

                    def project_c(ct):
                        if ct == 0:
                            pe.wait_ge(c_lo_done, count(t))
                            pe.wait_ge(we_lo_done, count(t))
                        three(z_ps[ct], lambda a, k: c_r[u][a][:, k, ct * P:(ct + 1) * P],
                              lambda b, k: we_r[u][b][:, k, :], False, False)

                    def project_rest(ct):
                        if ct == 0:
                            pe.wait_ge(w_lo_done, count(t))
                        three(z_ps[ct], lambda a, k: w_r[u][a][:, k, ct * P:(ct + 1) * P],
                              lambda b, k: (w3_hi, w3_lo)[b][:, k, :], False, False)
                        add_bias(z_ps[ct], 0).then_inc(z_done[ct], 1)

                    if live(t):
                        project_c2q(0)
                        project_c(0)
                        project_rest(0)
                    if live(t + 1):
                        pe.wait_ge(a_done, count(t + 1))
                        pe.wait_ge(g_mat_done, count(t + 1))
                        if begun(t):
                            pe.wait_ge(aT_copied, count(t))
                        for ct in range(CT):
                            ins = pe.transpose(aT_ps[0:NQ, ct * P:(ct + 1) * P], a_sb[:, ct, :], ident[:])
                        ins.then_inc(aTr_done, 1)
                        pe.wait_ge(diag_done, count(t + 1))
                        if begun(t):
                            pe.wait_ge(b_exp_done, count(t))
                        if live(t - 1):
                            pe.wait_ge(tanh_done, count(t - 1))
                        pe.matmul(bc_ps, ones[:], diag[:].rearrange("p c t -> p (c t)"), start=True,
                                  stop=True).then_inc(maxrow_done, 1)
                    if live(t):
                        project_c2q(1)
                        project_c(1)
                    if live(t + 2):
                        pe.wait_ge(q_in[u], pair * 16 + 32)
                        if begun(t + 1):
                            pe.wait_ge(g_mat_done, count(t + 1))
                        if begun(t + 1):
                            pe.wait_ge(aT_copied, count(t + 1))
                        for k in range(KT):
                            ins = pe.transpose(qT_ps[:, k, :], q_nat[u][:, k * P:(k + 1) * P], ident[0:NQ, 0:NQ])
                        ins.then_inc(qTr_done, 1)
                    if live(t):
                        project_rest(1)
                    if live(t - 1):
                        pe.wait_ge(leaves_done, count(t - 1))
                        pe.wait_ge(y2T_lo_done, count(t - 1))
                        for k in range(KT):
                            for ct in range(CT):
                                ins = pe.transpose(turned_ps[:, k, ct * P:(ct + 1) * P], leaf[:, ct, k * P:(k + 1) * P],
                                                   ident[:])
                        ins.then_inc(leafTr_done, 1)
                    if live(t + 1):
                        pe.wait_ge(aT_copied, count(t + 1))
                        if begun(t):
                            pe.wait_ge(u_lo_done, count(t))
                        if begun(t):
                            pe.wait_ge(w_done, count(t))
                        for k in range(KT):
                            ins = pe.matmul(c2q_ps[:, k, :], q_nat[v_][:, k * P:(k + 1) * P], aT[:], start=True, stop=True)
                        ins.then_inc(c2q_done, 1)
                    if live(t + 2):
                        pe.wait_ge(c_in[u], pair * 16 + 32)
                        pe.wait_ge(g_mat_done, count(t + 2))
                        if begun(t + 1):
                            pe.wait_ge(a_exp_done, count(t + 1))
                        for k in range(KT):
                            pe.matmul(s_ps, wq_rows[:, k, :], qT[:, k, :].unsqueeze(1).broadcast_to([P, CT, NQ]),
                                      start=(k == 0), stop=False)
                        for ct in range(CT):
                            for k in range(KT):
                                ins = pe.matmul(s_ps[:, ct, :], c[u][:, k, ct * P:(ct + 1) * P], g_mat[:, k, :],
                                                start=False, stop=(ct == CT - 1 and k == KT - 1))
                        ins.then_inc(scores_done, 1)
                    if live(t):
                        if begun(t - 1):
                            pe.wait_ge(lT_lo_done, count(t - 1))
                        for ct in range(CT):
                            pe.wait_ge(y2_done[ct], count(t))
                            for k in range(KT):
                                ins = pe.transpose(turned_ps[:, k, ct * P:(ct + 1) * P], y2[u][:, ct, k * P:(k + 1) * P],
                                                   ident[:])
                        ins.then_inc(y2Tr_done, 1)
                    if live(t - 1):
                        pe.wait_ge(lT_hi_done, count(t - 1))
                        pe.wait_ge(lT_lo_done, count(t - 1))
                        if begun(t - 2):
                            pe.wait_ge(res3_done, count(t - 2))
                        for ct in range(CT):
                            three(out_ps[:, ct, :], lambda a, k: (lT_hi, lT_lo)[a][:, k, ct * P:(ct + 1) * P],
                                  lambda b, k: (leafw_hi, leafw_lo)[b][:, k, :], True, False)
                            ins = add_bias(out_ps[:, ct, :], 1)
                        ins.then_inc(tree_done, 1)
                steps(pe, step)

            @block.scalar
            def _(act):
                def step(t, u, pair):
                    v_ = 1 - u
                    if live(t - 1):
                        act.wait_ge(gate_done, count(t - 1))
                        if begun(t - 2):
                            act.wait_ge(leaves_done, count(t - 2))
                        act.activation(th[:], gate_ps, ACT.Tanh, scale=0.5).then_inc(tanh_done, 1)
                    if live(t + 1):
                        act.wait_ge(sinv_done, count(t + 1))
                        for ct in range(CT):
                            ins = act.activation(a_sb[:, ct, :], a_sb[:, ct, :], ACT.Copy, scale=sinv[:, ct:ct + 1])
                        ins.then_inc(a_done, 1)
                        act.wait_ge(c_in[v_], (pair + u) * 16 + 16)
                        if begun(t - 1):
                            act.wait_ge(z_done[1], count(t - 1))
                        act.activation(c_r[v_][0][:], c[v_][:], ACT.Copy).then_inc(c_hi_done, 1)
                        act.wait_ge(aTr_done, count(t + 1))
                        if begun(t):
                            act.wait_ge(c2q_done, count(t))
                        act.activation(aT[:], aT_ps[0:NQ, :], ACT.Copy).then_inc(aT_copied, 1)
                        act.wait_ge(neg_m_done, count(t + 1))
                        if begun(t):
                            act.wait_ge(q2_done, count(t))
                        act.activation(eb[:], bc_ps, ACT.Exp, bias=neg_m[:], accum_out=ebsum[:]).then_inc(b_exp_done, 1)
                    if live(t + 2):
                        act.wait_ge(qTr_done, count(t + 2))
                        if begun(t + 1):
                            act.wait_ge(scores_done, count(t + 1))
                        act.activation(qT[:], qT_ps, ACT.Copy)
                        for k in range(KT):
                            ins = act.activation(g_mat[:, k, :], qT_ps[:, k, :], ACT.Identity, scale=vec3[:, 0, k:k + 1],
                                                 bias=vec3[:, 1, k:k + 1])
                        ins.then_inc(g_mat_done, 1)
                    if live(t - 1):
                        act.wait_ge(leafTr_done, count(t - 1))
                        if begun(t - 2):
                            act.wait_ge(tree_done, count(t - 2))
                        act.activation(lT_hi[:], turned_ps[:], ACT.Copy).then_inc(lT_hi_done, 1)
                    if live(t + 1):
                        act.wait_ge(c2q_done, count(t + 1))
                        act.activation(u_r[v_][0][:], c2q_ps[:], ACT.Copy).then_inc(u_hi_done, 1)
                    if live(t):
                        act.wait_ge(z_shift_done, count(t))
                        if begun(t - 2):
                            act.wait_ge(y2Tr_done, count(t - 2))
                        if begun(t - 2):
                            act.wait_ge(res3_done, count(t - 2))
                        for ct in range(CT):
                            act.activation(y2[u][:, ct, :], z_ps[ct], ACT.Identity, scale=rstd[0][:, ct:ct + 1],
                                           bias=shift[:, ct:ct + 1]).then_inc(y2_done[ct], 1)
                    if live(t):
                        act.wait_ge(y2Tr_done, count(t))
                        if begun(t - 1):
                            act.wait_ge(gate_done, count(t - 1))
                        act.activation(y2T_hi[:], turned_ps[:], ACT.Copy).then_inc(y2T_hi_done, 1)
                    if live(t + 1):
                        act.wait_ge(we_done, count(t + 1))
                        act.activation(we_r[v_][0][:], we32[:], ACT.Copy).then_inc(we_hi_done, 1)
                    if live(t + 2):
                        act.wait_ge(neg_smax_done, count(t + 2))
                        if begun(t + 1):
                            act.wait_ge(aTr_done, count(t + 1))
                        for ct in range(CT):
                            ins = act.activation(a_sb[:, ct, :], s_ps[:, ct, :], ACT.Exp, bias=neg_smax[:, ct:ct + 1],
                                                 accum_out=ssum[:, ct:ct + 1])
                        ins.then_inc(a_exp_done, 1)
                    if live(t + 1):
                        act.wait_ge(w_done, count(t + 1))
                        act.activation(w_r[v_][0][:], w32[:], ACT.Copy).then_inc(w_hi_done, 1)
                    if live(t + 2):
                        act.wait_ge(smax_done, count(t + 2))
                        if begun(t + 1):
                            act.wait_ge(maxrow_done, count(t + 1))
                        for ct in range(CT):
                            ins = act.activation(diag[:, ct, :], ident[:], ACT.Copy, scale=smax[:, ct:ct + 1])
                        ins.then_inc(diag_done, 1)

                steps(act, step)

            @block.vector
            def _(dve):
                def aggregate(n, b, stats_done, mean_done):
                    dve.wait_ge(s_ident, 1)
                    dve.wait_ge(stats_done, count(b))
                    for ct in range(CT):
                        ins = dve.bn_aggr(mv[n][:, ct, :], st[n][:, ct, :])
                    ins.then_inc(mean_done, 1)

                def add_eps(n, b, mean_done, var_done):
                    dve.wait_ge(mean_done, count(b))
                    dve.tensor_scalar(veps[n][:], mv[n][:, :, 1], EPS, None, ALU.add).then_inc(var_done, 1)

                def leaves(b, between):
                    dve.wait_ge(tanh_done, count(b))
                    dve.tensor_scalar(lv[0][:, :, 0:1], th[:, :, 0:1], -1.0, 1.0, ALU.mult, ALU.add)
                    dve.tensor_scalar(lv[0][:, :, 1:2], th[:, :, 0:1], 1.0, None, ALU.add).then_inc(level_done, 1)
                    src = lv[0]
                    for level in range(1, DEPTH):
                        n = 2 ** level
                        last = level == DEPTH - 1
                        if level in between:
                            between[level]()
                        if last:
                            if begun(b - 1):
                                dve.wait_ge(leafTr_done, count(b - 1))
                        dst = leaf if last else lv[level % 2]
                        kids = dst[:, :, 0:2 * n].rearrange("p c (m two) -> p c m two", two=2)
                        dve.wait_ge(level_done, b * NLV + level)
                        dve.scalar_tensor_tensor(kids[:, :, :, 0], th[:, :, n - 1:2 * n - 1], 1.0, src[:, :, 0:n],
                                                 ALU.subtract, ALU.mult, reverse0=True)
                        dve.scalar_tensor_tensor(kids[:, :, :, 1], th[:, :, n - 1:2 * n - 1], 1.0, src[:, :, 0:n],
                                                 ALU.add, ALU.mult).then_inc(leaves_done if last else level_done, 1)
                        src = dst

                def step(t, u, pair):
                    v_ = 1 - u
                    def out_stats(ct):
                        if live(t - 2):
                            dve.wait_ge(res3_done, count(t - 2))
                            ins = dve.bn_stats(st[1 + u][:, ct, :], r3[u][:, ct, :])
                            if ct == CT - 1:
                                ins.then_inc(r3_stats_done, 1)

                    def out_mean():
                        if live(t - 2):
                            aggregate(1 + u, t - 2, r3_stats_done, r3_mean_done)

                    def out_var():
                        if live(t - 2):
                            add_eps(1 + u, t - 2, r3_mean_done, r3_var_done)

                    def token_max():
                        if live(t + 1):
                            dve.wait_ge(maxrow_done, count(t + 1))
                            if begun(t):
                                dve.wait_ge(b_exp_done, count(t))
                            dve.tensor_reduce(neg_m[:], bc_ps, AX.X, ALU.max, negate=True).then_inc(neg_m_done, 1)

                    def z_stats():
                        if live(t):
                            dve.wait_ge(z_done[0], count(t))
                            dve.bn_stats(st[0][:, 0, :], z_ps[0])

                    if live(t - 1):
                        leaves(t - 1, {1: lambda: out_stats(0), 2: lambda: out_stats(1), 4: out_mean, 5: out_var,
                                       6: z_stats, 7: token_max})
                    else:
                        for ct in range(CT):
                            out_stats(ct)
                        out_mean()
                        out_var()
                        z_stats()
                        token_max()
                    if live(t):
                        dve.wait_ge(z_done[1], count(t))
                        dve.bn_stats(st[0][:, 1, :], z_ps[1]).then_inc(z_stats_done, 1)
                        aggregate(0, t, z_stats_done, z_mean_done)
                        add_eps(0, t, z_mean_done, z_var_done)
                    if live(t + 1):
                        dve.wait_ge(b_exp_done, count(t + 1))
                        for k in range(KT):
                            ins = dve.tensor_tensor_reduce(scratch[:, k, :], c[v_][:, k, :], eb[:], 1.0, 0.0, ALU.mult,
                                                           ALU.add, q2_raw[:, k:k + 1])
                        ins.then_inc(q2_sum_done, 1)
                    if live(t + 1):
                        dve.reciprocal(ebinv[:], ebsum[:]).then_inc(eb_inv_done, 1)
                    if live(t):
                        dve.wait_ge(rstd2_done, count(t))
                        if begun(t - 1):
                            dve.wait_ge(y2_done[1], count(t - 1))
                        dve.scalar_tensor_tensor(shift[:], mv[0][:, :, 0], -1.0, rstd[0][:], ALU.mult, ALU.mult)\
                            .then_inc(z_shift_done, 1)
                    if live(t + 1):
                        dve.wait_ge(eb_inv_done, count(t + 1))
                        dve.wait_ge(q2_sum_done, count(t + 1))
                        dve.tensor_scalar(q2[:], q2_raw[:], ebinv[:], None, ALU.mult).then_inc(q2_done, 1)
                    if live(t - 1):
                        dve.wait_ge(lT_hi_done, count(t - 1))
                        dve.tensor_tensor(lT_lo[:], turned_ps[:], f(lT_hi[:]), ALU.subtract).then_inc(lT_lo_done, 1)
                    if live(t + 1):
                        dve.wait_ge(q2_done, count(t + 1))
                        if begun(t):
                            dve.wait_ge(we_lo_done, count(t))
                        for k in range(KT):
                            ins = dve.scalar_tensor_tensor(we32[:, k, :], wl_raw[:, 3, k, :], q2[:, k:k + 1],
                                                           w1_id[:, k, :], ALU.mult, ALU.add)
                        ins.then_inc(we_done, 1)
                    if live(t + 2):
                        dve.wait_ge(scores_done, count(t + 2))
                        if begun(t + 1):
                            dve.wait_ge(a_exp_done, count(t + 1))
                        dve.tensor_reduce(neg_smax[:], s_ps, AX.X, ALU.max, negate=True).then_inc(neg_smax_done, 1)
                    if live(t):
                        dve.wait_ge(y2T_hi_done, count(t))
                        dve.tensor_tensor(y2T_lo[:], turned_ps[:], f(y2T_hi[:]), ALU.subtract).then_inc(y2T_lo_done, 1)
                    if live(t + 1):
                        dve.wait_ge(u_hi_done, count(t + 1))
                        if begun(t):
                            dve.wait_ge(w_lo_done, count(t))
                        dve.tensor_tensor(w32[:], c2q_ps[:], c[v_][:], ALU.mult).then_inc(w_done, 1)
                        dve.tensor_tensor(u_r[v_][1][:], c2q_ps[:], f(u_r[v_][0][:]), ALU.subtract).then_inc(u_lo_done, 1)
                    if live(t + 2):
                        dve.wait_ge(neg_smax_done, count(t + 2))
                        if begun(t + 1):
                            dve.wait_ge(diag_done, count(t + 1))
                        dve.tensor_scalar(smax[:], neg_smax[:], -1.0, const[:], ALU.mult, ALU.add).then_inc(smax_done, 1)
                    if live(t + 2):
                        dve.wait_ge(a_exp_done, count(t + 2))
                        dve.reciprocal(sinv[:], ssum[:]).then_inc(sinv_done, 1)
                    if live(t - 1):
                        dve.wait_ge(tree_done, count(t - 1))
                        if begun(t - 3):
                            dve.wait_ge(y3_done, count(t - 3))
                        dve.tensor_tensor(r3[v_][:], out_ps[:], y2[v_][:], ALU.add).then_inc(res3_done, 1)

                steps(dve, step)

            @block.gpsimd
            def _(pool):
                def step(t, u, pair):
                    v_ = 1 - u
                    if live(t):
                        pool.wait_ge(z_var_done, count(t))
                        if begun(t - 1):
                            pool.wait_ge(y2_done[1], count(t - 1))
                        pool.tensor_tensor(rstd[0][:], veps[0][:], neg_half[:], ALU.pow).then_inc(rstd2_done, 1)
                    if live(t + 1):
                        pool.wait_ge(c_hi_done, count(t + 1))
                        pool.tensor_tensor(c_r[v_][1][:], c[v_][:], f(c_r[v_][0][:]), ALU.subtract).then_inc(c_lo_done, 1)
                    if live(t + 1):
                        pool.wait_ge(we_hi_done, count(t + 1))
                        pool.tensor_tensor(we_r[v_][1][:], we32[:], f(we_r[v_][0][:]), ALU.subtract)\
                            .then_inc(we_lo_done, 1)
                        pool.wait_ge(w_hi_done, count(t + 1))
                        pool.tensor_tensor(w_r[v_][1][:], w32[:], f(w_r[v_][0][:]), ALU.subtract).then_inc(w_lo_done, 1)
                    if live(t - 2):
                        if above_zero(pair - 1 - 1):
                            pool.wait_ge(y_out[u], pair * (16 * CT) - 16 * CT)
                        pool.wait_ge(r3_var_done, count(t - 2))
                        pool.tensor_tensor(rstd[1 + u][:], veps[1 + u][:], neg_half[:], ALU.pow).then_inc(rstd3_done, 1)
                        pool.wait_ge(s_ident, 1)
                        pool.wait_ge(rstd3_done, count(t - 2))
                        for ct in range(CT):
                            ins = pool.tensor_scalar(y3[u][:, ct, :], r3[u][:, ct, :], mv[1 + u][:, ct, 0:1],
                                                     rstd[1 + u][:, ct:ct + 1], ALU.subtract, ALU.mult)
                        ins.then_inc(y3_done, 1)

                steps(pool, step)


_INS = ["x", "ctx_1024", "L0_attn_Wq", "L0_attn_Wkv", "L0_attn_Wo", "L0_xattn_w_cq", "L0_xattn_b_cq", "L0_xattn_w_c",
        "L0_xattn_b_c", "L0_xattn_w_q", "L0_xattn_b_q", "L0_xattn_W_l", "L0_xattn_b_l", "L0_ffn_Wq",
        "L0_ffn_routers", "L0_ffn_leaf_values", "L0_ffn_Wout_w", "L0_ffn_Wout_b"]
_TRANSPOSED = ("L0_xattn_W_l", "L0_ffn_routers", "L0_ffn_leaf_values", "L0_ffn_Wout_w")


def kernel(**inputs):
    import numpy as _np
    import concourse.bacc as _bacc
    from concourse import mybir as _mybir
    from concourse.bass_utils import run_bass_kernel_spmd as _run

    nc = _bacc.Bacc("TRN2", target_bir_lowering=False, num_devices=1)
    arrays, args = {}, []
    for name in _INS:
        a = _np.asarray(inputs[name])
        if name in _TRANSPOSED:
            a = a.T
        if a.ndim == 0:
            a = a.reshape(1)
        a = _np.ascontiguousarray(a)
        arrays[f"in_{name}_dram"] = a
        args.append(nc.dram_tensor(f"in_{name}_dram", a.shape, _mybir.dt.from_np(a.dtype), kind="ExternalInput").ap())
    res = nc.dram_tensor("out_0_dram", (L, NB, D), F32, kind="ExternalOutput").ap()
    decoder_layer(nc, *args, res)
    r = _run(nc, [arrays], core_ids=[0])
    return r.results[0]["out_0_dram"]
```
